# Optimizing a Trainium2 kernel written in Bass

```python
import numpy as np
import jax
import jax.numpy as jnp

def _softmax(x, axis=-1):
    return jax.nn.softmax(x, axis=axis)

def _gelu(x):
    return jax.nn.gelu(x, approximate=True)

def _silu(x):
    return jax.nn.silu(x)

def _sigmoid(x):
    return jax.nn.sigmoid(x)

def _layernorm(x, axis=-1, eps=1e-05):
    m = jnp.mean(x, axis=axis, keepdims=True)
    v = jnp.var(x, axis=axis, keepdims=True)
    return (x - m) / jnp.sqrt(v + eps)

def _scatter_add(tgt, idx, src, axis=0):
    return tgt.at[idx].add(src)

def _segment_sum(src, seg, n):
    return jax.ops.segment_sum(src, seg, n)
kernel_name = 'mk_metaformer_d1_conv_nhwc512_r4_12a823'

def setup_inputs(seed: int=0):
    np.random.seed(seed)
    _w = jnp.asarray

    def _rec_inputs():
        import jax
        import jax.numpy as jnp
        _gk = jax.random.key(seed)
        x = -0.0003929 + 0.9999 * jax.random.normal(jax.random.fold_in(_gk, 1), (2, 16, 64, 128), jnp.float32)
        return x
    x = _rec_inputs()

    def _L0_conv_setup():
        import jax, jax.numpy as jnp
        import numpy as np
        DIM = 128
        DEPTH = 4
        HEADS = 8
        DIM_HEAD = 16
        INNER = HEADS * DIM_HEAD
        LN_EPS = 1e-05

        def _rotary(x):
            n, dh = (x.shape[-2], x.shape[-1])
            inv_freq = 1.0 / 10000.0 ** (jnp.arange(0, dh, 2, dtype=jnp.float32) / dh)
            freqs = jnp.arange(n, dtype=jnp.float32)[:, None] * inv_freq[None, :]
            freqs = jnp.repeat(freqs, 2, axis=-1)
            cos, sin = (jnp.cos(freqs), jnp.sin(freqs))
            x1 = x[..., 0::2]
            x2 = x[..., 1::2]
            x_rot = jnp.stack((-x2, x1), axis=-1).reshape(x.shape)
            return x * cos + x_rot * sin

        def _layernorm(x, g, b):
            mu = jnp.mean(x, axis=-1, keepdims=True)
            var = jnp.mean(jnp.square(x - mu), axis=-1, keepdims=True)
            return (x - mu) * jax.lax.rsqrt(var + LN_EPS) * g + b

        def _attention(x, w_qkv, w_out, b_out):
            B, n, _ = x.shape
            qkv = x @ w_qkv
            q, k, v = jnp.split(qkv, 3, axis=-1)

            def to_heads(t):
                return t.reshape(B, n, HEADS, DIM_HEAD).transpose(0, 2, 1, 3)
            q, k, v = (to_heads(q), to_heads(k), to_heads(v))
            q = _rotary(q)
            k = _rotary(k)
            scale = DIM_HEAD ** (-0.5)
            attn = jax.nn.softmax(jnp.einsum('bhid,bhjd->bhij', q, k) * scale, axis=-1)
            out = jnp.einsum('bhij,bhjd->bhid', attn, v)
            out = out.transpose(0, 2, 1, 3).reshape(B, n, INNER)
            return out @ w_out + b_out
        key = jax.random.key(seed)
        ks = jax.random.split(key, 8)
        b, t, p = (2, 16, 64)
        x = jax.random.normal(ks[0], (b, t, p, DIM), dtype=jnp.float32)
        std = 0.02
        inp = {'x': x, 'ln_s_g': jnp.ones((DEPTH, DIM), jnp.float32), 'ln_s_b': jnp.zeros((DEPTH, DIM), jnp.float32), 'w_qkv_s': jax.random.normal(ks[1], (DEPTH, DIM, 3 * INNER), jnp.float32) * std, 'w_out_s': jax.random.normal(ks[2], (DEPTH, INNER, DIM), jnp.float32) * std, 'b_out_s': jnp.zeros((DEPTH, DIM), jnp.float32), 'ln_t_g': jnp.ones((DEPTH, DIM), jnp.float32), 'ln_t_b': jnp.zeros((DEPTH, DIM), jnp.float32), 'w_qkv_t': jax.random.normal(ks[3], (DEPTH, DIM, 3 * INNER), jnp.float32) * std, 'w_out_t': jax.random.normal(ks[4], (DEPTH, INNER, DIM), jnp.float32) * std, 'b_out_t': jnp.zeros((DEPTH, DIM), jnp.float32), 'ln_f_g': jnp.ones((DEPTH, DIM), jnp.float32), 'ln_f_b': jnp.zeros((DEPTH, DIM), jnp.float32)}
        return inp
    _L0_conv_all = _L0_conv_setup()
    _L0_conv_in = {k: v for k, v in _L0_conv_all.items() if k in ('ln_s_g', 'ln_s_b', 'w_qkv_s', 'w_out_s', 'b_out_s', 'ln_t_g', 'ln_t_b', 'w_qkv_t', 'w_out_t', 'b_out_t', 'ln_f_g', 'ln_f_b')}
    del _L0_conv_all

    def _L0_ffn_setup():
        import jax, jax.numpy as jnp
        import numpy as np
        B, T, D, F, E, TOP_K = (8, 1024, 128, 512, 8, 2)

        def _moe_forward(x, Wr, W1, W2):
            b, t, d = x.shape
            e = Wr.shape[1]
            xf = x.reshape(-1, d)
            n = xf.shape[0]
            logits = xf @ Wr
            probs = jax.nn.softmax(logits, axis=-1)
            w, idx = jax.lax.top_k(probs, TOP_K)
            w = w.astype(xf.dtype)
            gates = jnp.zeros((n, e), xf.dtype).at[jnp.arange(n)[:, None], idx].add(w)

            def body(acc, expert):
                w1, w2, g = expert
                h = jax.nn.gelu(xf @ w1, approximate=False)
                return (acc + g[:, None] * (h @ w2), None)
            out, _ = jax.lax.scan(body, jnp.zeros_like(xf), (W1, W2, gates.T))
            return out.reshape(b, t, d)
        key = jax.random.key(seed)
        k1, k2, k3, k4 = jax.random.split(key, 4)
        x = jax.random.normal(k1, (B, T, D), jnp.float32)
        Wr = jax.random.normal(k2, (D, E), jnp.float32) * (1.0 / np.sqrt(D))
        W1 = jax.random.normal(k3, (E, D, F), jnp.float32) * (1.0 / np.sqrt(D))
        W2 = jax.random.normal(k4, (E, F, D), jnp.float32) * (1.0 / np.sqrt(F))
        return {'x': x, 'Wr': Wr, 'W1': W1, 'W2': W2}
    _L0_ffn_all = _L0_ffn_setup()
    _L0_ffn_in = {k: v for k, v in _L0_ffn_all.items() if k in ('Wr', 'W1', 'W2')}
    del _L0_ffn_all
    return {'x': x, 'L0_conv_ln_s_g': _L0_conv_in['ln_s_g'], 'L0_conv_ln_s_b': _L0_conv_in['ln_s_b'], 'L0_conv_w_qkv_s': _L0_conv_in['w_qkv_s'], 'L0_conv_w_out_s': _L0_conv_in['w_out_s'], 'L0_conv_b_out_s': _L0_conv_in['b_out_s'], 'L0_conv_ln_t_g': _L0_conv_in['ln_t_g'], 'L0_conv_ln_t_b': _L0_conv_in['ln_t_b'], 'L0_conv_w_qkv_t': _L0_conv_in['w_qkv_t'], 'L0_conv_w_out_t': _L0_conv_in['w_out_t'], 'L0_conv_b_out_t': _L0_conv_in['b_out_t'], 'L0_conv_ln_f_g': _L0_conv_in['ln_f_g'], 'L0_conv_ln_f_b': _L0_conv_in['ln_f_b'], 'L0_ffn_Wr': _L0_ffn_in['Wr'], 'L0_ffn_W1': _L0_ffn_in['W1'], 'L0_ffn_W2': _L0_ffn_in['W2']}

def reference(x, L0_conv_ln_s_g, L0_conv_ln_s_b, L0_conv_w_qkv_s, L0_conv_w_out_s, L0_conv_b_out_s, L0_conv_ln_t_g, L0_conv_ln_t_b, L0_conv_w_qkv_t, L0_conv_w_out_t, L0_conv_b_out_t, L0_conv_ln_f_g, L0_conv_ln_f_b, L0_ffn_Wr, L0_ffn_W1, L0_ffn_W2):
    import jax
    import jax.numpy as jnp

    def _L0_conv_ref(x, ln_s_g, ln_s_b, w_qkv_s, w_out_s, b_out_s, ln_t_g, ln_t_b, w_qkv_t, w_out_t, b_out_t, ln_f_g, ln_f_b):
        import jax, jax.numpy as jnp
        import numpy as np
        DIM = 128
        DEPTH = 4
        HEADS = 8
        DIM_HEAD = 16
        INNER = HEADS * DIM_HEAD
        LN_EPS = 1e-05

        def _rotary(x):
            n, dh = (x.shape[-2], x.shape[-1])
            inv_freq = 1.0 / 10000.0 ** (jnp.arange(0, dh, 2, dtype=jnp.float32) / dh)
            freqs = jnp.arange(n, dtype=jnp.float32)[:, None] * inv_freq[None, :]
            freqs = jnp.repeat(freqs, 2, axis=-1)
            cos, sin = (jnp.cos(freqs), jnp.sin(freqs))
            x1 = x[..., 0::2]
            x2 = x[..., 1::2]
            x_rot = jnp.stack((-x2, x1), axis=-1).reshape(x.shape)
            return x * cos + x_rot * sin

        def _layernorm(x, g, b):
            mu = jnp.mean(x, axis=-1, keepdims=True)
            var = jnp.mean(jnp.square(x - mu), axis=-1, keepdims=True)
            return (x - mu) * jax.lax.rsqrt(var + LN_EPS) * g + b

        def _attention(x, w_qkv, w_out, b_out):
            B, n, _ = x.shape
            qkv = x @ w_qkv
            q, k, v = jnp.split(qkv, 3, axis=-1)

            def to_heads(t):
                return t.reshape(B, n, HEADS, DIM_HEAD).transpose(0, 2, 1, 3)
            q, k, v = (to_heads(q), to_heads(k), to_heads(v))
            q = _rotary(q)
            k = _rotary(k)
            scale = DIM_HEAD ** (-0.5)
            attn = jax.nn.softmax(jnp.einsum('bhid,bhjd->bhij', q, k) * scale, axis=-1)
            out = jnp.einsum('bhij,bhjd->bhid', attn, v)
            out = out.transpose(0, 2, 1, 3).reshape(B, n, INNER)
            return out @ w_out + b_out
        b, t, p, d = x.shape
        for i in range(DEPTH):
            xs = x.reshape(b * t, p, d)
            xs = _layernorm(xs, ln_s_g[i], ln_s_b[i])
            x_s = _attention(xs, w_qkv_s[i], w_out_s[i], b_out_s[i]).reshape(b, t, p, d)
            xt = (x + x_s).transpose(0, 2, 1, 3).reshape(b * p, t, d)
            xt = _layernorm(xt, ln_t_g[i], ln_t_b[i])
            x_t = _attention(xt, w_qkv_t[i], w_out_t[i], b_out_t[i])
            x_t = x_t.reshape(b, p, t, d).transpose(0, 2, 1, 3)
            x = _layernorm(x_s + x_t, ln_f_g[i], ln_f_b[i]) + x
        return x

    def _L0_ffn_ref(x, Wr, W1, W2):
        import jax, jax.numpy as jnp
        import numpy as np
        B, T, D, F, E, TOP_K = (8, 1024, 128, 512, 8, 2)

        def _moe_forward(x, Wr, W1, W2):
            b, t, d = x.shape
            e = Wr.shape[1]
            xf = x.reshape(-1, d)
            n = xf.shape[0]
            logits = xf @ Wr
            probs = jax.nn.softmax(logits, axis=-1)
            w, idx = jax.lax.top_k(probs, TOP_K)
            w = w.astype(xf.dtype)
            gates = jnp.zeros((n, e), xf.dtype).at[jnp.arange(n)[:, None], idx].add(w)

            def body(acc, expert):
                w1, w2, g = expert
                h = jax.nn.gelu(xf @ w1, approximate=False)
                return (acc + g[:, None] * (h @ w2), None)
            out, _ = jax.lax.scan(body, jnp.zeros_like(xf), (W1, W2, gates.T))
            return out.reshape(b, t, d)
        return _moe_forward(x, Wr, W1, W2)

    def _gn(v, G=32, eps=1e-05):
        B_, H_, W_, C_ = v.shape
        g = v.reshape(B_, H_, W_, G, C_ // G)
        m = jnp.mean(g, axis=(1, 2, 4), keepdims=True)
        s = jnp.var(g, axis=(1, 2, 4), keepdims=True)
        return ((g - m) / jnp.sqrt(s + eps)).reshape(v.shape)

    def _ln_c(v, eps=1e-06):
        m = jnp.mean(v, axis=-1, keepdims=True)
        s = jnp.var(v, axis=-1, keepdims=True)
        return (v - m) / jnp.sqrt(s + eps)

    def _ln_t(v, eps=1e-05):
        m = jnp.mean(v, axis=-1, keepdims=True)
        s = jnp.var(v, axis=-1, keepdims=True)
        return (v - m) / jnp.sqrt(s + eps)

    def _to_tokens(v):
        B_, H_, W_, C_ = v.shape
        return v.reshape(B_, H_ * W_, C_)

    def _from_tokens(t, like):
        return t.reshape(like.shape)
    x = x + _L0_conv_ref(_ln_c(x), L0_conv_ln_s_g, L0_conv_ln_s_b, L0_conv_w_qkv_s, L0_conv_w_out_s, L0_conv_b_out_s, L0_conv_ln_t_g, L0_conv_ln_t_b, L0_conv_w_qkv_t, L0_conv_w_out_t, L0_conv_b_out_t, L0_conv_ln_f_g, L0_conv_ln_f_b)
    t = _to_tokens(x)
    t = t + _L0_ffn_ref(_ln_t(t), L0_ffn_Wr, L0_ffn_W1, L0_ffn_W2)
    x = _from_tokens(t, x)
    return x

_drawn_inputs = setup_inputs


def setup_inputs(seed=0):
    import zlib

    import numpy as np

    out = dict(_drawn_inputs(seed))
    spreads = {'L0_conv_ln_s_g': (1.0, 0.2),
     'L0_conv_ln_s_b': (0.0, 0.333),
     'L0_conv_b_out_s': (0.0, 0.1),
     'L0_conv_ln_t_g': (1.0, 0.2),
     'L0_conv_ln_t_b': (0.0, 0.341),
     'L0_conv_b_out_t': (0.0, 0.1),
     'L0_conv_ln_f_g': (1.0, 0.2),
     'L0_conv_ln_f_b': (0.0, 0.1)}
    factors = {}
    for name, (base, spread) in spreads.items():
        noise = np.random.default_rng([zlib.crc32(name.encode()), seed]).standard_normal(out[name].shape)
        drawn = base * np.exp(spread * noise) if base else spread * noise
        out[name] = jnp.asarray(drawn.astype(out[name].dtype))
    for name, factor in factors.items():
        out[name] = (out[name] * factor).astype(out[name].dtype)
    return out
```

```python
from contextlib import ExitStack

import concourse.bass as bass
from concourse import mybir

ALU = mybir.AluOpType
ACT = mybir.ActivationFunctionType
F32 = mybir.dt.float32
BF16 = mybir.dt.bfloat16
AX_X = mybir.AxisListType.X

P = 128
BATCH, TIME, PATCH = 2, 16, 64
TOKENS = BATCH * TIME * PATCH
CHUNKS = TOKENS // P
HC = CHUNKS // BATCH
HT = TOKENS // BATCH
DEPTH, HEADS, DH = 4, 8, 16
PAIRS = HEADS // 2
BANK = 512
VW = DH + 1
EXPERTS, FF = 8, 512
FC = FF // P
CONV_EPS, NORM_EPS = 1e-6, 1e-5
SCALE = DH ** -0.5

WQ, WK, WQS, WKS, WV, WO, GAMMA, BETA, WCOLS = 0, 128, 256, 384, 512, 640, 768, 769, 770


class Branch:

    def __init__(self, name, block, groups):
        self.name = name
        self.block = block
        self.blocks = P // block
        self.parts = P // block
        self.groups = groups
        self.group_chunks = HC // groups


SPATIAL = Branch("s", 64, 2)
TEMPORAL = Branch("t", 32, 1)

STEPS = [
    ("norm", SPATIAL, 0, 0), ("project", SPATIAL, 0, 0), ("norm", SPATIAL, 1, 0),
    ("score", SPATIAL, 0, 0), ("project", SPATIAL, 1, 0), ("mix", SPATIAL, 0, 0),
    ("score", SPATIAL, 0, 1), ("score_end", SPATIAL, 0, 1), ("mix", SPATIAL, 0, 1),
    ("score", SPATIAL, 1, 0), ("out", SPATIAL, 0, 0), ("mix", SPATIAL, 1, 0),
    ("score", SPATIAL, 1, 1), ("norm", TEMPORAL, 0, 0), ("mix", SPATIAL, 1, 1),
    ("project", TEMPORAL, 0, 0), ("out", SPATIAL, 1, 0),
    ("score", TEMPORAL, 0, 0), ("norm", TEMPORAL, 1, 0), ("project", TEMPORAL, 1, 0),
    ("mix", TEMPORAL, 0, 0), ("score", TEMPORAL, 1, 0), ("out", TEMPORAL, 0, 0),
    ("final", TEMPORAL, 0, 0), ("mix", TEMPORAL, 1, 0), ("out", TEMPORAL, 1, 0),
    ("final", TEMPORAL, 1, 0),
]
STEPS = [s for s in STEPS if s[0] != "score_end"]


def uses(step, br):
    return {
        "norm": (0, 0, 2, 0), "project": (8, 0, 0, 2), "score": (0, 1, 0, 0),
        "mix": (0, 0, 4, 2 if br is SPATIAL else 4), "out": (0, 0, 2, 2), "final": (0, 0, 0, 0),
    }[step]


def numbered():
    at = [0, 0, 0, 0]
    out = []
    for step, br, half, grp in STEPS:
        out.append((step, br, half, grp, tuple(at)))
        at = [a + u for a, u in zip(at, uses(step, br))]
    return out


PLAN = numbered()


def nth(step, br, half, grp=0):
    return [s[:4] for s in PLAN if s[0] == step].index((step, br, half, grp))


def metaformer(nc, x, w_s, w_t, vec_in, rope_s, rope_t, headmask, ident_in, pairmask,
               router, w1, w2, out):
    ctx = ExitStack()
    with ctx:
        def sb(name, shape, dt=F32):
            return ctx.enter_context(nc.sbuf_tensor(name, shape, dt))

        def sem(name):
            return ctx.enter_context(nc.semaphore(name))

        x_in = sb("x_in", [P, CHUNKS, P])
        x_res = sb("x_res", [P, CHUNKS, P])
        x_bias = sb("x_bias", [P, CHUNKS, P])
        x_mid = sb("x_mid", [P, CHUNKS, P])
        x_sum = sb("x_sum", [P, CHUNKS, P])
        x_nrm = sb("x_nrm", [P, CHUNKS, P])
        raw = x_nrm
        xnT = sb("xnT", [P, TOKENS])
        qT = sb("qT", [P, TOKENS])
        kE = sb("kE", [P, 2, TOKENS])
        kR = sb("kR", [P, 2, BANK])
        rope1 = sb("rope1", [P, 4, BANK])
        rope2 = sb("rope2", [P, 4, BANK])
        v_s = sb("v_s", [P, 32, PAIRS, 2 * VW])
        v_t = sb("v_t", [P, 32, PAIRS, 4 * VW])
        prob = sb("prob", [P, 2, PAIRS, 4, P])
        probT = sb("probT", [P, 2, 4, PAIRS, P])
        top = sb("top", [P, 2, 4 * BANK // 32])
        den = sb("den", [P, 2, 16])
        o_nrm = sb("o_nrm", [P, 8, 2 * P])
        oT = xnT
        ws = sb("ws", [P, WCOLS])
        wt = sb("wt", [P, WCOLS])
        vec = sb("vec", [P, 4, P])
        b_both = sb("b_both", [P, P])
        cs_s = sb("cs_s", [P, 2, PATCH])
        cs_t = sb("cs_t", [P, 2, TIME])
        hmask = sb("hmask", [P, 2])
        ident = sb("ident", [P, P])
        pmask = sb("pmask", [2, P + BANK], BF16)
        stats = sb("stats", [P, 2, HC, 6])
        mv = sb("mv", [P, 2, HC, 2])
        nmean = sb("nmean", [P, 2, HC])
        veps = sb("veps", [P, 2, HC])
        rstd = sb("rstd", [P, 2, HC])
        mhalf = sb("mhalf", [P, HC])
        rt = sb("rt", [P, EXPERTS])
        w1_sb = v_t[:, 0:16, :, :].rearrange("p a b c -> p (a b c)")[:, 0:2 * FF].rearrange("p (s n) -> p s n", s=2)
        w2_sb = v_s[:, :, :, :].rearrange("p a b c -> p (a b c)")[:, 0:2 * FF].rearrange("p (s c n) -> p s c n", s=2, c=FC)
        hid = prob[:, :, :, :, :].rearrange("p s g k n -> p s g (k n)")
        gate = sb("gate", [P, CHUNKS, 2, EXPERTS // 2])
        lg = sb("lg", [P, CHUNKS, EXPERTS])
        lmax = sb("lmax", [P, CHUNKS])
        lsum = sb("lsum", [P, CHUNKS])
        prb = sb("prb", [P, CHUNKS, EXPERTS])
        above = rope1[:, 0:2, :].rearrange("p a b -> p (a b)").rearrange("p (c e f) -> p c e f", c=CHUNKS, e=EXPERTS)
        ties = rope2[:, 0:2, :].rearrange("p a b -> p (a b)").rearrange("p (c e f) -> p c e f", c=CHUNKS, e=EXPERTS)
        before = sb("before", [P, EXPERTS, EXPERTS])
        rank = sb("rank", [P, CHUNKS, EXPERTS])

        score = ctx.enter_context(nc.psum_tensor("score", [P, 4, BANK], F32))
        turn = ctx.enter_context(nc.psum_tensor("turn", [P, 2, BANK], F32))
        small = ctx.enter_context(nc.psum_tensor("small", [P, 2, BANK], F32))

        loaded = sem("loaded")
        x_loaded = sem("x_loaded")
        ready = sem("ready")
        stat_done = sem("stat_done")
        mv_ready = sem("mv_ready")
        nrm_step = sem("nrm_step")
        nrm_ready = sem("nrm_ready")
        turn_full = sem("turn_full")
        turn_free = [sem(f"turn_free{i}") for i in range(2)]
        small_full = sem("small_full")
        small_free = [sem(f"small_free{i}") for i in range(2)]
        proj_full = sem("proj_full")
        proj_free = sem("proj_free")
        rope_free = sem("rope_free")
        kr_ready = sem("kr_ready")
        qk_ready = sem("qk_ready")
        score_full = sem("score_full")
        top_ready = sem("top_ready")
        score_free = sem("score_free")
        prob_ready = sem("prob_ready")
        den_ready = sem("den_ready")
        bias_ready = sem("bias_ready")
        mid_ready = sem("mid_ready")
        sum_ready = sem("sum_ready")
        fin_step = sem("fin_step")
        wt_loaded = sem("wt_loaded")
        vec_loaded = sem("vec_loaded")
        ws_loaded = sem("ws_loaded")
        s_out_done = sem("s_out_done")
        m_a = sem("m_a")
        m_lg = sem("m_lg")
        m_sub = sem("m_sub")
        m_exp = sem("m_exp")
        w_loaded = [sem(f"w_loaded{i}") for i in range(2)]
        h_full = sem("h_full")
        h_free = sem("h_free")
        y_full = sem("y_full")
        y_free = sem("y_free")
        stored = sem("stored")
        arrived = sem("arrived")
        go = sem("go")
        left = sem("left")

        LAYER_SEMS = [stat_done, mv_ready, nrm_step, nrm_ready, turn_full, *turn_free, small_full, *small_free,
                      proj_full, proj_free, rope_free, kr_ready, qk_ready, score_full, top_ready, score_free,
                      prob_ready, den_ready, bias_ready, mid_ready, sum_ready, fin_step,
                      wt_loaded, vec_loaded, ws_loaded, s_out_done]
        EXPERT_SEMS = [*w_loaded, h_full, h_free, y_full, y_free]

        def turn_end(eng):
            eng.drain().then_inc(arrived, 1)
            eng.wait_ge(go, 1)
            eng.drain().then_inc(left, 1)

        def turn_clear(sp, sems, engines):
            sp.wait_ge(arrived, engines)
            sp.drain()
            for s in (*sems, arrived):
                sp.sem_clear(s)
            sp.drain().then_inc(go, 1)
            sp.wait_ge(left, engines)
            sp.drain()
            sp.sem_clear(go)
            sp.sem_clear(left)
            sp.drain()

        def chunks_of(t, half):
            return t[:, half * HC:(half + 1) * HC, :]

        block = ctx.enter_context(nc.Block())

        @block.sync
        def _(sp):
            sp.dma_start(x_in[:, :, :], x).then_inc(x_loaded, 16)
            for dst, src in ((ws[:, :], w_s[0]), (ident[:, :], ident_in), (cs_s[:, :, :], rope_s),
                             (cs_t[:, :, :], rope_t), (hmask[:, :], headmask), (pmask[:, :], pairmask),
                             (rt[:, :], router)):
                sp.dma_start(dst, src).then_inc(loaded, 16)
            turn_clear(sp, [stat_done, mv_ready, nrm_step, nrm_ready], 4)
            with sp.Fori(0, DEPTH) as layer:
                sp.dma_start(wt[:, :], w_t[bass.ds(layer, 1)].rearrange("o p n -> p (o n)")).then_inc(wt_loaded, 16)
                sp.dma_start(vec[:, :, :], vec_bcast(vec_in, layer)).then_inc(vec_loaded, 16)
                sp.wait_ge(s_out_done, 1)
                sp.dma_start(ws[:, :], w_s[bass.ds(layer + 1, 1)].rearrange("o p n -> p (o n)")).then_inc(ws_loaded, 16)
                sp.wait_ge(wt_loaded, 16)
                sp.wait_ge(vec_loaded, 16)
                sp.wait_ge(ws_loaded, 16)
                turn_clear(sp, LAYER_SEMS, 4)
            with sp.Fori(0, EXPERTS // 2) as pair:
                for s in range(2):
                    sp.dma_start(w1_sb[:, s, :], w1.rearrange("(q s) p n -> q s p n", s=2)[bass.ds(pair, 1), s].rearrange("o p n -> p (o n)")).then_inc(w_loaded[s], 16)
                    sp.dma_start(w2_sb[:, s, :, :], w2.rearrange("(q s) p c n -> q s p c n", s=2)[bass.ds(pair, 1), s].rearrange("o p c n -> p (o c) n")).then_inc(w_loaded[s], 16)
                for s in range(2):
                    sp.wait_ge(w_loaded[s], 32)
                turn_clear(sp, EXPERT_SEMS, 3)
            sp.dma_start(out, x_in[:, :, :]).then_inc(stored, 16)
            sp.wait_ge(stored, 16)

        @block.gpsimd
        def _(pool):
            nc.gpsimd.memset(mhalf[:, :], -0.5).then_inc(ready, 1)
            nc.gpsimd.memset(v_s[:, :, :, :], 0.0).then_inc(ready, 1)
            nc.gpsimd.memset(v_t[:, :, :, :], 0.0).then_inc(ready, 1)

            def inverse_std(s, eps, stepped, n):
                nc.gpsimd.tensor_scalar(veps[:, s, :], mv[:, s, :, 1], eps, 1.0, ALU.add, ALU.mult).then_inc(stepped, 1)
                nc.gpsimd.tensor_scalar(nmean[:, s, :], mv[:, s, :, 0], -1.0, 0.0, ALU.mult, ALU.add).then_inc(stepped, 1)
                pool.wait_ge(stepped, n + 1)
                nc.gpsimd.tensor_tensor(rstd[:, s, :], veps[:, s, :], mhalf[:, :], ALU.pow).then_inc(stepped, 1)
                pool.wait_ge(stepped, n + 3)
                return n + 3

            def normalise(dst, src, half, s):
                for c in range(HC):
                    k = half * HC + c
                    last = nc.gpsimd.tensor_scalar(dst[:, k, :], src[:, k, :], nmean[:, s, c:c + 1],
                                                   rstd[:, s, c:c + 1], ALU.add, ALU.mult)
                return last

            n = 0
            for half in range(BATCH):
                pool.wait_ge(mv_ready, half + 1)
                n = inverse_std(half, CONV_EPS, nrm_step, n)
                normalise(x_res, x_in, half, half).then_inc(nrm_ready, 1)
            turn_end(pool)

            with pool.Fori(0, DEPTH):
                pool.wait_ge(vec_loaded, 16)
                nc.gpsimd.tensor_tensor(b_both[:, :], vec[:, 0, :], vec[:, 1, :], ALU.add).then_inc(bias_ready, 1)
                for half in range(BATCH):
                    nc.gpsimd.tensor_tensor(chunks_of(x_bias, half), chunks_of(x_res, half),
                                            vec[:, 0:1, :].broadcast_to([P, HC, P]), ALU.add).then_inc(bias_ready, 1)
                pool.wait_ge(bias_ready, 3)
                n = 0
                tile = 0
                f = 0
                for step, br, half, grp, (pj, sc, tn, sm) in PLAN:
                    if step == "norm":
                        i = nth("norm", br, half)
                        pool.wait_ge(mv_ready, i + 1)
                        n = inverse_std(i % 2, NORM_EPS, nrm_step, n)
                        normalise(x_nrm, x_res if br is SPATIAL else x_mid, half, i % 2).then_inc(nrm_ready, 1)
                    elif step == "project":
                        for t in range(2):
                            cols = slice(half * HT + t * BANK, half * HT + (t + 1) * BANK)
                            pool.wait_ge(proj_free, 4 * tile + 2)
                            nc.gpsimd.tensor_tensor(qT[:, cols], rope1[:, (2 * tile) % 4, :], rope2[:, (2 * tile) % 4, :],
                                                    ALU.add).then_inc(rope_free, 1)
                            pool.wait_ge(proj_free, 4 * tile + 4)
                            nc.gpsimd.tensor_tensor(kR[:, tile % 2, :], rope1[:, (2 * tile + 1) % 4, :],
                                                    rope2[:, (2 * tile + 1) % 4, :], ALU.add).then_inc(rope_free, 1)
                            pool.wait_ge(rope_free, 2 * tile + 2)
                            for e in range(2):
                                last = nc.gpsimd.tensor_scalar(kE[:, e, cols], kR[:, tile % 2, :], hmask[:, e:e + 1], 1.0,
                                                               ALU.mult, ALU.mult)
                            last.then_inc(qk_ready, 1)
                            tile += 1
                    elif step == "out" and br is SPATIAL:
                        for u in (sm, sm + 1):
                            pool.wait_ge(small_free[u % 2], u // 2 + 1)
                        nc.gpsimd.tensor_tensor(chunks_of(x_mid, half), chunks_of(raw, half), chunks_of(x_bias, half),
                                                ALU.add).then_inc(mid_ready, 1)
                        nc.gpsimd.tensor_tensor(chunks_of(x_sum, half), chunks_of(raw, half),
                                                b_both[:, None, :].broadcast_to([P, HC, P]), ALU.add).then_inc(sum_ready, 1)
                    elif step == "final":
                        i = 4 + half
                        pool.wait_ge(mv_ready, i + 1)
                        nc.gpsimd.tensor_tensor(chunks_of(x_bias, half), chunks_of(x_res, half),
                                                vec[:, 3:4, :].broadcast_to([P, HC, P]), ALU.add).then_inc(fin_step, 1)
                        n = inverse_std(i % 2, NORM_EPS, nrm_step, n)
                        normalise(x_nrm, x_sum, half, i % 2).then_inc(fin_step, 1)
                        pool.wait_ge(fin_step, f + 2)
                        nc.gpsimd.tensor_tensor(chunks_of(raw, half), chunks_of(x_nrm, half),
                                                vec[:, 2:3, :].broadcast_to([P, HC, P]), ALU.mult).then_inc(fin_step, 1)
                        pool.wait_ge(fin_step, f + 3)
                        nc.gpsimd.tensor_tensor(chunks_of(x_res, half), chunks_of(raw, half), chunks_of(x_bias, half),
                                                ALU.add).then_inc(fin_step, 1)
                        f += 4
                turn_end(pool)

            for half in range(BATCH):
                nc.gpsimd.tensor_tensor(chunks_of(x_in, half), chunks_of(x_in, half), chunks_of(x_res, half),
                                        ALU.add).then_inc(mid_ready, 1)
            n = 0
            for half in range(BATCH):
                pool.wait_ge(mv_ready, half + 1)
                n = inverse_std(half, NORM_EPS, nrm_step, n)
                normalise(x_nrm, x_in, half, half).then_inc(nrm_ready, 1)

        @block.scalar
        def _(act):
            act.wait_ge(loaded, 16 * 7)
            act.wait_ge(ready, 9)
            turn_end(act)

            with act.Fori(0, DEPTH):
                for step, br, half, grp, (pj, sc, tn, sm) in PLAN:
                    w = ws if br is SPATIAL else wt
                    if step == "norm":
                        if br is TEMPORAL:
                            act.wait_ge(wt_loaded, 16)
                        for t in range(2):
                            u = tn + t
                            act.wait_ge(turn_full, u + 1)
                            src = turn[:, u % 2, :]
                            dst = xnT[:, half * HT + t * BANK:half * HT + (t + 1) * BANK]
                            if br is TEMPORAL:
                                src = src.rearrange("d (t p) -> d p t", p=PATCH)
                                dst = xnT[:, half * HT:(half + 1) * HT].rearrange("d (p t) -> d p t", t=TIME)[
                                    :, :, t * 8:(t + 1) * 8]
                            nc.scalar.activation(dst, src, ACT.Identity, bias=w[:, BETA:BETA + 1],
                                                 scale=w[:, GAMMA:GAMMA + 1]).then_inc(turn_free[u % 2], 1)
                    elif step == "project":
                        v = v_s if br is SPATIAL else v_t
                        for t in range(2):
                            u = sm + t
                            act.wait_ge(small_full, u + 1)
                            b0 = half * 16 + t * 8
                            for i in range(br.parts):
                                rows = slice(i * br.block, (i + 1) * br.block)
                                src = small[rows, u % 2, :].rearrange("p (u g d) -> p u g d", u=8, d=DH)
                                last = nc.scalar.activation(v[rows, b0:b0 + 8, :, i * VW:i * VW + DH], src, ACT.Copy)
                            last.then_inc(small_free[u % 2], 1)
                    elif step == "score":
                        i = sc
                        for h in range(2):
                            act.wait_ge(score_free, 2 * i + h + 1)
                            p = prob[:, i % 2, :, 2 * h:2 * h + 2, :].rearrange("p g k n -> p g (k n)")
                            nc.scalar.activation(p, p, ACT.Exp, scale=SCALE).then_inc(prob_ready, 1)
                    elif step == "mix":
                        i = nth("mix", br, half, grp)
                        for k in range(0, 4, 2):
                            u = tn + k
                            act.wait_ge(turn_full, u + 1)
                            nc.scalar.activation(probT[:, i % 2, k, :, :].rearrange("p g n -> p (g n)"),
                                                 turn[:, u % 2, :], ACT.Copy).then_inc(turn_free[u % 2], 1)
                    elif step == "out":
                        for t in range(2):
                            u = tn + t
                            act.wait_ge(turn_full, u + 1)
                            src = turn[:, u % 2, :]
                            dst = oT[:, half * HT + t * BANK:half * HT + (t + 1) * BANK]
                            if br is TEMPORAL:
                                src = src.rearrange("d (p t) -> d t p", t=TIME)
                                dst = oT[:, half * HT:(half + 1) * HT].rearrange("d (t p) -> d t p", p=PATCH)[
                                    :, :, t * 32:(t + 1) * 32]
                            nc.scalar.activation(dst, src, ACT.Copy).then_inc(turn_free[u % 2], 1)
                        if br is SPATIAL:
                            for t in range(2):
                                u = sm + t
                                act.wait_ge(small_full, u + 1)
                                c0 = half * HC + 4 * t
                                nc.scalar.activation(raw[:, c0:c0 + 4, :].rearrange("p c n -> p (c n)"), small[:, u % 2, :],
                                                     ACT.Copy).then_inc(small_free[u % 2], 1)
                turn_end(act)

            for t in range(4):
                act.wait_ge(turn_full, t + 1)
                nc.scalar.activation(xnT[:, t * BANK:(t + 1) * BANK], turn[:, t % 2, :], ACT.Copy).then_inc(turn_free[t % 2], 1)
            act.wait_ge(m_sub, 1)
            nc.scalar.activation(prb[:, :, :], lg[:, :, :], ACT.Exp).then_inc(m_exp, 1)

            with act.Fori(0, EXPERTS // 2):
                n = 0
                for s in range(2):
                    for t in range(4):
                        if n >= 2:
                            act.wait_ge(y_full, n - 1)
                        for c in range(FC):
                            act.wait_ge(h_full, n * FC + c + 1)
                            nc.scalar.activation(hid[:, n % 2, c, :], score[:, c, :], ACT.Gelu).then_inc(h_free, 1)
                        n += 1
                turn_end(act)

        @block.tensor
        def _(pe):
            pe.wait_ge(loaded, 16 * 7)
            turn_end(pe)

            def to_features(src_chunks, u, wait=True):
                if wait and u >= 2:
                    pe.wait_ge(turn_free[u % 2], u // 2)
                for j, src in enumerate(src_chunks):
                    last = nc.tensor.transpose(turn[:, u % 2, j * P:(j + 1) * P], src, ident[:, :])
                last.then_inc(turn_full, 1)

            def small_bank(u):
                if u >= 2:
                    pe.wait_ge(small_free[u % 2], u // 2)
                return small[:, u % 2, :]

            with pe.Fori(0, DEPTH):
                for step, br, half, grp, (pj, sc, tn, sm) in PLAN:
                    w = ws if br is SPATIAL else wt
                    n = br.block
                    if step == "norm":
                        pe.wait_ge(nrm_ready, nth("norm", br, half) + 1)
                        for t in range(2):
                            c0 = half * HC + 4 * t
                            to_features([x_nrm[:, c, :] for c in range(c0, c0 + 4)], tn + t)
                    elif step == "project":
                        if br is TEMPORAL:
                            pe.wait_ge(wt_loaded, 16)
                        last_norm = [q for q in PLAN if q[:3] == ("norm", br, half)][0][4][2]
                        for u in (last_norm, last_norm + 1):
                            pe.wait_ge(turn_free[u % 2], u // 2 + 1)
                        if sc:
                            pe.wait_ge(score_free, 2 * sc)
                        for t in range(2):
                            cols = xnT[:, half * HT + t * BANK:half * HT + (t + 1) * BANK]
                            for j, off in enumerate((WQ, WQS, WK, WKS)):
                                i = pj + 4 * t + j
                                if i >= 4:
                                    pe.wait_ge(proj_free, i - 3)
                                nc.tensor.matmul(score[:, j, :], w[:, off:off + P], cols, start=True,
                                                 stop=True).then_inc(proj_full, 1)
                        for t in range(2):
                            bank = small_bank(sm + t)
                            for v in range(8):
                                b = half * 16 + t * 8 + v
                                for i in range(br.parts):
                                    if br is SPATIAL:
                                        tok = b * n
                                    else:
                                        tok = (2 * (b // 4) + i // 2) * P + (b % 4) * n
                                    h = i % 2
                                    last = nc.tensor.matmul(bank[i * n:(i + 1) * n, v * 64:(v + 1) * 64], xnT[:, tok:tok + n],
                                                            w[:, WV + 64 * h:WV + 64 * h + 64], start=True, stop=True)
                            last.then_inc(small_full, 1)
                    elif step == "score":
                        done = [q for q in PLAN[:PLAN.index((step, br, half, grp, (pj, sc, tn, sm)))] if q[0] == "project"]
                        pe.wait_ge(qk_ready, 2 * (nth("project", br, half) + 1))
                        pe.wait_ge(proj_free, 8 * len(done))
                        if sc:
                            pe.wait_ge(score_free, 2 * sc)
                        if br is TEMPORAL:
                            for g in range(PAIRS):
                                nc.tensor.matmul(score[:, g, :], pmask[:, 0:P], pmask[:, P:P + BANK], start=True, stop=False,
                                                 skip_group_check=True)
                        for c in range(br.group_chunks):
                            chunk = half * HC + grp * br.group_chunks + c
                            for b in range(br.blocks):
                                tok = chunk * P + b * n
                                for g in range(PAIRS):
                                    rows = slice(32 * g, 32 * g + 32)
                                    last = nc.tensor.matmul(
                                        score[b * n:(b + 1) * n, g, c * 2 * n:(c + 1) * 2 * n], qT[rows, tok:tok + n],
                                        kE[rows, :, tok:tok + n], start=br is SPATIAL, stop=True,
                                        skip_group_check=br is TEMPORAL, tile_position=(32 * g, b * n))
                        last.then_inc(score_full, 1)
                    elif step == "mix":
                        i = nth("mix", br, half, grp)
                        v = v_s if br is SPATIAL else v_t

                        def turned(k):
                            if k % 2 == 0:
                                pe.wait_ge(prob_ready, 2 * i + k // 2 + 1)
                            to_features([prob[:, i % 2, g, k, :] for g in range(PAIRS)], tn + k)

                        def weighted(k):
                            u = tn + k
                            pe.wait_ge(turn_free[u % 2], u // 2 + 1)
                            if br is SPATIAL:
                                unit, first, last_of = sm + k // 2, k % 2 == 0, k % 2 == 1
                                blk0 = (half * HC + grp * 4 + k) * 2
                            else:
                                unit, first, last_of = sm + k, True, True
                                blk0 = half * 16 + k * 4
                            bank = small_bank(unit) if first else small[:, unit % 2, :]
                            if k == 0:
                                pv = [q for q in PLAN if q[:3] == ("project", br, half)][0][4][3]
                                for z in (pv, pv + 1):
                                    pe.wait_ge(small_free[z % 2], z // 2 + 1)
                            cols = bank[:, 0:16 * VW].rearrange("p (c g w) -> p c g w", c=2, g=PAIRS)
                            if br is SPATIAL:
                                cols = cols[:, k % 2:k % 2 + 1, :, :]
                            for b in range(br.blocks):
                                for g in range(PAIRS):
                                    last = nc.tensor.matmul(
                                        cols[b * n:(b + 1) * n, :, g, :],
                                        probT[:, i % 2, k, g, b * n:(b + 1) * n], v[:, blk0 + b, g, :], start=True, stop=True)
                            if last_of:
                                last.then_inc(small_full, 1)

                        turned(0)
                        turned(1)
                        weighted(0)
                        turned(2)
                        weighted(1)
                        turned(3)
                        weighted(2)
                        weighted(3)
                    elif step == "out":
                        before = [q for q in PLAN if q[:3] == ("mix", br, half)]
                        units = [q[4][3] + z for q in before for z in range(uses("mix", br)[3])]
                        for z in units[-2:]:
                            pe.wait_ge(small_free[z % 2], z // 2 + 1)
                        for t in range(2):
                            srcs = []
                            for j in range(4):
                                c = 4 * t + j
                                srcs.append(o_nrm[:, half * 4 + c // 2, (c % 2) * P:(c % 2 + 1) * P])
                            to_features(srcs, tn + t)
                        for u in (tn, tn + 1):
                            pe.wait_ge(turn_free[u % 2], u // 2 + 1)
                        for t in range(2):
                            bank = small_bank(sm + t)
                            for j in range(4):
                                c = half * HC + 4 * t + j
                                last = nc.tensor.matmul(bank[:, j * P:(j + 1) * P], oT[:, c * P:(c + 1) * P], w[:, WO:WO + P],
                                                        start=True, stop=True)
                            last.then_inc(small_full, 1)
                        if br is SPATIAL and half == 1:
                            pe.wait_ge(small_full, sm + 2)
                            pe.drain().then_inc(s_out_done, 1)
                turn_end(pe)

            for t in range(4):
                pe.wait_ge(nrm_ready, t // 2 + 1)
                to_features([x_nrm[:, c, :] for c in range(4 * t, 4 * t + 4)], t)
            pe.wait_ge(turn_free[0], 2)
            pe.wait_ge(turn_free[1], 2)
            for c in range(CHUNKS):
                last = nc.tensor.matmul(small[:, 0, c * EXPERTS:(c + 1) * EXPERTS], xnT[:, c * P:(c + 1) * P], rt[:, :],
                                        start=True, stop=True)
            last.then_inc(m_lg, 1)

            with pe.Fori(0, EXPERTS // 2):
                def second(n):
                    if n >= 2:
                        pe.wait_ge(y_free, n - 1)
                    for j in range(4):
                        for c in range(FC):
                            if j == 0:
                                pe.wait_ge(h_free, n * FC + c + 1)
                            last = nc.tensor.matmul(small[:, n % 2, j * P:(j + 1) * P], hid[:, n % 2, c, j * P:(j + 1) * P],
                                                    w2_sb[:, n // 4, c, :], start=c == 0, stop=c == FC - 1)
                    last.then_inc(y_full, 1)

                for n in range(8):
                    pe.wait_ge(w_loaded[n // 4], 32)
                    for c in range(FC):
                        if n >= 1:
                            pe.wait_ge(h_free, (n - 1) * FC + c + 1)
                        nc.tensor.matmul(score[:, c, :], w1_sb[:, n // 4, c * P:(c + 1) * P],
                                         xnT[:, (n % 4) * BANK:(n % 4 + 1) * BANK], start=True, stop=True).then_inc(h_full, 1)
                    if n >= 1:
                        second(n - 1)
                second(7)
                turn_end(pe)

        @block.vector
        def _(dve):
            def moments(src, half, s, done, ready_sem, n):
                for c in range(HC):
                    nc.vector.bn_stats(stats[:, s, c, :], src[:, half * HC + c, :]).then_inc(done, 1)
                dve.wait_ge(done, n + HC)
                for c in range(HC):
                    last = nc.vector.bn_aggr(mv[:, s, c, :], stats[:, s, c, :])
                last.then_inc(ready_sem, 1)
                return n + HC

            dve.wait_ge(x_loaded, 16)
            n = 0
            for half in range(BATCH):
                n = moments(x_in, half, half, stat_done, mv_ready, n)
            dve.wait_ge(ready, 3)
            for br, v in ((SPATIAL, v_s), (TEMPORAL, v_t)):
                for i in range(br.parts):
                    nc.vector.memset(v[i * br.block:(i + 1) * br.block, :, :, i * VW + DH:(i + 1) * VW], 1.0).then_inc(ready, 1)
            turn_end(dve)

            with dve.Fori(0, DEPTH):
                n = 0
                units = 0
                for step, br, half, grp, (pj, sc, tn, sm) in PLAN:
                    if step == "norm":
                        if br is TEMPORAL:
                            dve.wait_ge(mid_ready, half + 1)
                        i = nth("norm", br, half)
                        if i >= 2:
                            dve.wait_ge(nrm_ready, i - 1)
                        n = moments(x_res if br is SPATIAL else x_mid, half, i % 2, stat_done, mv_ready, n)
                    elif step == "project":
                        table = cs_s if br is SPATIAL else cs_t
                        length = PATCH if br is SPATIAL else TIME
                        for j in range(8):
                            i = pj + j
                            r = i // 2
                            dst = (rope1 if i % 2 == 0 else rope2)[:, r % 4, :]
                            if r >= 4:
                                dve.wait_ge(rope_free, r - 3)
                            dve.wait_ge(proj_full, i + 1)
                            rep = BANK // length
                            nc.vector.tensor_tensor(
                                dst.rearrange("p (s n) -> p s n", n=length),
                                score[:, i % 4, :].rearrange("p (s n) -> p s n", n=length),
                                table[:, i % 2, None, :].broadcast_to([P, rep, length]), ALU.mult).then_inc(proj_free, 1)
                    elif step == "score":
                        i = sc
                        rows = 4 * BANK // br.block
                        dve.wait_ge(score_full, i + 1)
                        nc.vector.tensor_reduce(top[:, i % 2, 0:rows],
                                                score[:, :, :].rearrange("p g (r n) -> p (g r) n", n=br.block),
                                                AX_X, ALU.max).then_inc(top_ready, 1)
                        dve.wait_ge(top_ready, i + 1)
                        per = BANK // br.block
                        for h in range(2):
                            tops = top[:, i % 2, 0:rows].rearrange("p (g r) -> p g r", g=PAIRS)[:, :, h * per // 2:(h + 1) * per // 2]
                            nc.vector.tensor_tensor(
                                prob[:, i % 2, :, 2 * h:2 * h + 2, :].rearrange("p g k (r n) -> p g (k r) n", n=br.block),
                                score[:, :, h * 256:(h + 1) * 256].rearrange("p g (r n) -> p g r n", n=br.block),
                                tops[:, :, :, None].broadcast_to([P, PAIRS, per // 2, br.block]),
                                ALU.subtract).then_inc(score_free, 1)
                    elif step == "mix":
                        i = nth("mix", br, half, grp)
                        def copied(k):
                            u = tn + k
                            dve.wait_ge(turn_full, u + 1)
                            nc.vector.tensor_copy(probT[:, i % 2, k, :, :].rearrange("p g n -> p (g n)"),
                                                  turn[:, u % 2, :]).then_inc(turn_free[u % 2], 1)

                        def divided(z):
                            u = sm + z
                            dve.wait_ge(small_full, u + 1)
                            src = small[:, u % 2, 0:16 * VW].rearrange("p (h d) -> p h d", d=VW)
                            nc.vector.reciprocal(den[:, u % 2, :], src[:, :, DH]).then_inc(den_ready, 1)
                            dve.wait_ge(den_ready, unit0 + z + 1)
                            slot = half * 4 + (grp * 2 + z)
                            nc.vector.tensor_tensor(o_nrm[:, slot, :].rearrange("p (h d) -> p h d", d=DH), src[:, :, 0:DH],
                                                    den[:, u % 2, :, None].broadcast_to([P, 16, DH]),
                                                    ALU.mult).then_inc(small_free[u % 2], 1)

                        unit0 = units
                        copied(1)
                        if br is TEMPORAL:
                            divided(0)
                            divided(1)
                            copied(3)
                            divided(2)
                            divided(3)
                            units += 4
                        else:
                            copied(3)
                            divided(0)
                            divided(1)
                            units += 2
                    elif step == "out" and br is TEMPORAL:
                        dve.wait_ge(sum_ready, half + 1)
                        for t in range(2):
                            u = sm + t
                            c0 = half * HC + 4 * t
                            dve.wait_ge(small_full, u + 1)
                            z = x_sum[:, c0:c0 + 4, :].rearrange("p c n -> p (c n)")
                            nc.vector.tensor_tensor(z, small[:, u % 2, :], z, ALU.add).then_inc(small_free[u % 2], 1)
                            dve.wait_ge(small_free[u % 2], u // 2 + 1)
                    elif step == "final":
                        i = 4 + half
                        dve.wait_ge(nrm_ready, 4)
                        n = moments(x_sum, half, i % 2, stat_done, mv_ready, n)
                turn_end(dve)

            n = 0
            for half in range(BATCH):
                dve.wait_ge(mid_ready, half + 1)
                n = moments(x_in, half, half, stat_done, mv_ready, n)

            chain = [0]

            def link(ins):
                chain[0] += 1
                ins.then_inc(m_a, 1)
                dve.wait_ge(m_a, chain[0])

            link(nc.vector.memset(before[:, :, :], 0.0))
            for e in range(1, EXPERTS):
                last = nc.vector.memset(before[:, e, 0:e], 1.0)
                last.then_inc(m_a, 1)
                chain[0] += 1
            dve.wait_ge(m_a, chain[0])
            dve.wait_ge(m_lg, 1)
            logits = small[:, 0, 0:CHUNKS * EXPERTS].rearrange("p (c e) -> p c e", e=EXPERTS)
            link(nc.vector.tensor_reduce(lmax[:, :], logits, AX_X, ALU.max))
            nc.vector.tensor_tensor(lg[:, :, :], logits, lmax[:, :, None].broadcast_to([P, CHUNKS, EXPERTS]),
                                    ALU.subtract).then_inc(m_sub, 1)
            dve.wait_ge(m_exp, 1)
            link(nc.vector.tensor_reduce(lsum[:, :], prb[:, :, :], AX_X, ALU.add))
            link(nc.vector.reciprocal(lmax[:, :], lsum[:, :]))
            link(nc.vector.tensor_tensor(lg[:, :, :], prb[:, :, :], lmax[:, :, None].broadcast_to([P, CHUNKS, EXPERTS]), ALU.mult))
            mine = lg[:, :, :, None].broadcast_to([P, CHUNKS, EXPERTS, EXPERTS])
            others = lg[:, :, None, :].broadcast_to([P, CHUNKS, EXPERTS, EXPERTS])
            link(nc.vector.tensor_tensor(above, others, mine, ALU.is_gt))
            link(nc.vector.tensor_tensor(ties, others, mine, ALU.is_equal))
            link(nc.vector.tensor_tensor(ties, ties, before[:, None, :, :].broadcast_to([P, CHUNKS, EXPERTS, EXPERTS]), ALU.mult))
            link(nc.vector.tensor_tensor(above, above, ties, ALU.add))
            link(nc.vector.tensor_reduce(rank[:, :, :], above, AX_X, ALU.add))
            link(nc.vector.tensor_scalar(rank[:, :, :], rank[:, :, :], 1.5, None, ALU.is_lt))
            link(nc.vector.tensor_tensor(gate[:, :, :, :].rearrange("p c s q -> p c q s"), lg[:, :, :].rearrange("p c (q s) -> p c q s", s=2),
                                         rank[:, :, :].rearrange("p c (q s) -> p c q s", s=2), ALU.mult))

            with dve.Fori(0, EXPERTS // 2) as pair:
                for n in range(8):
                    dve.wait_ge(y_full, n + 1)
                    for j in range(4):
                        c = (n % 4) * 4 + j
                        last = nc.vector.scalar_tensor_tensor(
                            out=x_in[:, c, :], in0=small[:, n % 2, j * P:(j + 1) * P],
                            scalar=gate[:, c, n // 4, bass.ds(pair, 1)], in1=x_in[:, c, :], op0=ALU.mult, op1=ALU.add)
                    last.then_inc(y_free, 1)
                turn_end(dve)


def vec_bcast(vec_in, layer):
    row = vec_in[bass.ds(layer, 1)]
    return row.broadcast_to([P, 4, P])


def rope_table(length):
    import numpy as np
    freq = (1.0 / np.float32(10000.0) ** (np.arange(0, DH, 2, dtype=np.float32) / np.float32(DH))).astype(np.float32)
    angle = (np.arange(length, dtype=np.float32)[:, None] * freq[None, :]).astype(np.float32)
    angle = np.repeat(angle, 2, axis=-1).T
    sign = np.where(np.arange(DH) % 2 == 0, -1.0, 1.0)[:, None]
    cos = np.tile(np.cos(angle.astype(np.float64)), (HEADS, 1))
    sin = np.tile(np.sin(angle.astype(np.float64)) * sign, (HEADS, 1))
    return np.ascontiguousarray(np.stack([cos, sin], axis=1).astype(np.float32))


def kernel(**inputs):
    import numpy as np
    import concourse.bacc as bacc
    from concourse.bass_utils import run_bass_kernel_spmd

    a = {k: np.asarray(v) for k, v in inputs.items()}

    def packed(tag):
        qkv = a[f"L0_conv_w_qkv_{tag}"]
        q, k, v = qkv[:, :, 0:P], qkv[:, :, P:2 * P], qkv[:, :, 2 * P:3 * P]
        swap = np.arange(P) ^ 1
        v = v.reshape(DEPTH, P, PAIRS, 2, DH).transpose(0, 1, 3, 2, 4).reshape(DEPTH, P, P)
        w = np.concatenate([q, k, q[:, :, swap], k[:, :, swap], v, a[f"L0_conv_w_out_{tag}"],
                            a[f"L0_conv_ln_{tag}_g"][:, :, None], a[f"L0_conv_ln_{tag}_b"][:, :, None]], axis=2)
        return np.ascontiguousarray(w)

    w_s = packed("s")
    w_s = np.concatenate([w_s, w_s[:1]], axis=0)
    parity = np.zeros((2, P + BANK), np.float32)
    for r in range(2):
        parity[r, 0:P] = (np.arange(P) // TIME) % 2 == r
        parity[r, P:] = np.where((np.arange(BANK) // TIME) % 2 == r, 0.0, -1e30)
    import ml_dtypes
    arrays = {
        "x": np.ascontiguousarray(a["x"].reshape(CHUNKS, P, P).transpose(1, 0, 2)),
        "w_s": np.ascontiguousarray(w_s),
        "w_t": packed("t"),
        "vec_in": np.ascontiguousarray(np.stack([a["L0_conv_b_out_s"], a["L0_conv_b_out_t"], a["L0_conv_ln_f_g"],
                                                 a["L0_conv_ln_f_b"]], axis=1)),
        "rope_s": rope_table(PATCH),
        "rope_t": rope_table(TIME),
        "headmask": np.ascontiguousarray(np.stack([(np.arange(P) // DH) % 2 == e for e in range(2)], axis=1).astype(np.float32)),
        "ident": np.eye(P, dtype=np.float32),
        "pairmask": parity.astype(ml_dtypes.bfloat16),
        "router": np.ascontiguousarray(a["L0_ffn_Wr"]),
        "w1": np.ascontiguousarray(a["L0_ffn_W1"]),
        "w2": np.ascontiguousarray(a["L0_ffn_W2"].reshape(EXPERTS, FC, P, P).transpose(0, 2, 1, 3)),
    }
    nc = bacc.Bacc("TRN2", target_bir_lowering=False, num_devices=1)
    args = [nc.dram_tensor(f"in_{k}", v.shape, mybir.dt.from_np(v.dtype), kind="ExternalInput").ap()
            for k, v in arrays.items()]
    out = nc.dram_tensor("out_x", (P, CHUNKS, P), F32, kind="ExternalOutput").ap()
    metaformer(nc, *args, out)
    r = run_bass_kernel_spmd(nc, [{f"in_{k}": v for k, v in arrays.items()}], core_ids=[0])
    got = r.results[0]["out_x"]
    return np.ascontiguousarray(got.transpose(1, 0, 2)).reshape(BATCH, TIME, PATCH, P)
```

```python
from contextlib import ExitStack

import concourse.bass as bass
from concourse import mybir

ALU = mybir.AluOpType
ACT = mybir.ActivationFunctionType
F32 = mybir.dt.float32
BF16 = mybir.dt.bfloat16
AX_X = mybir.AxisListType.X

P = 128
BATCH, TIME, PATCH = 2, 16, 64
TOKENS = BATCH * TIME * PATCH
CHUNKS = TOKENS // P
HC = CHUNKS // BATCH
HT = TOKENS // BATCH
DEPTH, HEADS, DH = 4, 8, 16
PAIRS = HEADS // 2
BANK = 512
VW = DH + 1
EXPERTS, FF = 8, 512
FC = FF // P
CONV_EPS, NORM_EPS = 1e-6, 1e-5
SCALE = DH ** -0.5

WQ, WK, WQS, WKS, WV, WO, GAMMA, BETA, WCOLS = 0, 128, 256, 384, 512, 640, 768, 769, 770


class Branch:

    def __init__(self, name, block, groups):
        self.name = name
        self.block = block
        self.blocks = P // block
        self.parts = P // block
        self.groups = groups
        self.group_chunks = HC // groups


SPATIAL = Branch("s", 64, 2)
TEMPORAL = Branch("t", 32, 1)

S, T, C, F, E = "s", "t", "c", "f", "e"


def layer_steps(n):
    p = n - 1
    lead = [("head", p, T, 1, 0)] if n else []
    before = [("mix", p, T, 1, 0), ("divide", p, T, 1, 0)] if n else []
    after = [("divide", p, T, 1, 1), ("out", p, T, 1, 0), ("stats", p, F, 1, 0)] if n else []
    ended = [("normal", p, F, 1, 0)] if n else []
    then = [("stats", n + 1, S, 0, 0)] if n + 1 < DEPTH else []
    onward = [("normal", n + 1, S, 0, 0)] if n + 1 < DEPTH else []
    turn = [("turn", n + 1, S, 0, 0)] if n + 1 < DEPTH else []
    ahead = [("project", n + 1, S, 0, 0), ("values", n + 1, S, 0, 0)] if n + 1 < DEPTH else []
    return [
        *lead, ("score", n, S, 0, 0), ("most", n, S, 0, 0), *before, ("less", n, S, 0, 0), *after,
        ("bias", n, S, 0, 0), ("head", n, S, 0, 0), ("score", n, S, 0, 1), ("most", n, S, 0, 1),
        ("mix", n, S, 0, 0), ("less", n, S, 0, 1), ("divide", n, S, 0, 0), *ended, ("stats", n, S, 1, 0),
        ("bias", n, S, 1, 0), ("head", n, S, 0, 1), ("mix", n, S, 0, 1), ("divide", n, S, 0, 1),
        ("normal", n, S, 1, 0), ("out", n, S, 0, 0), ("stats", n, T, 0, 0),
        ("turn", n, S, 1, 0), ("project", n, S, 1, 0), ("normal", n, T, 0, 0), ("bias", n, F, 0, 0),
        ("turn", n, T, 0, 0), ("project", n, T, 0, 0), ("values", n, S, 1, 0),
        ("score", n, S, 1, 0), ("most", n, S, 1, 0), ("values", n, T, 0, 0), ("less", n, S, 1, 0),
        ("head", n, S, 1, 0), ("score", n, S, 1, 1), ("most", n, S, 1, 1), ("mix", n, S, 1, 0),
        ("less", n, S, 1, 1), ("divide", n, S, 1, 0), ("head", n, S, 1, 1), ("score", n, T, 0, 0),
        ("most", n, T, 0, 0), ("mix", n, S, 1, 1), ("divide", n, S, 1, 1), ("less", n, T, 0, 0),
        ("out", n, S, 1, 0), ("stats", n, T, 1, 0), ("head", n, T, 0, 0), ("mix", n, T, 0, 0),
        ("divide", n, T, 0, 0), ("divide", n, T, 0, 1), ("normal", n, T, 1, 0), ("bias", n, F, 1, 0),
        ("out", n, T, 0, 0), ("stats", n, F, 0, 0), ("turn", n, T, 1, 0), ("project", n, T, 1, 0),
        ("normal", n, F, 0, 0), *then, ("values", n, T, 1, 0), ("score", n, T, 1, 0), *onward,
        ("most", n, T, 1, 0), *turn, ("less", n, T, 1, 0), *ahead,
    ]


def all_steps():
    last = DEPTH - 1
    steps = [("stats", 0, C, 0, 0), ("stats", 0, C, 1, 0), ("normal", 0, C, 0, 0), ("stats", 0, S, 0, 0),
             ("normal", 0, C, 1, 0), ("normal", 0, S, 0, 0), ("turn", 0, S, 0, 0), ("project", 0, S, 0, 0),
             ("values", 0, S, 0, 0)]
    for n in range(DEPTH):
        steps += layer_steps(n)
    steps += [("stats", last, E, 0, 0), ("head", last, T, 1, 0), ("mix", last, T, 1, 0), ("divide", last, T, 1, 0),
              ("divide", last, T, 1, 1), ("normal", last, E, 0, 0), ("out", last, T, 1, 0),
              ("stats", last, F, 1, 0), ("turn", last, E, 0, 0), ("normal", last, F, 1, 0), ("stats", last, E, 1, 0),
              ("normal", last, E, 1, 0), ("turn", last, E, 1, 0)]
    return steps


USES = {"project": (8, 0, 0, 0), "values": (0, 0, 0, 2), "score": (0, 1, 0, 0), "turn": (0, 0, 2, 0),
        "head": (0, 0, 2, 0), "out": (0, 0, 2, 2)}


class Step:

    def __init__(self, key, nth, used):
        self.step, self.layer, self.kind, self.half, self.group = key
        self.nth = nth
        self.proj, self.scores, self.turns, self.smalls = used


def numbered():
    used, seen, out = [0, 0, 0, 0], {}, {}
    for key in all_steps():
        step, kind = key[0], key[2]
        out[key] = Step(key, seen.get(step, 0), used)
        seen[step] = seen.get(step, 0) + 1
        takes = (0, 0, 2, 2 if kind == S else 4) if step == "mix" else USES.get(step, (0, 0, 0, 0))
        used = [a + b for a, b in zip(used, takes)]
    return out


STEPS = numbered()
PLAN = list(STEPS.values())
BRANCH = {S: SPATIAL, T: TEMPORAL}


def metaformer(nc, x, w_s, w_t, vec_in, rope_s, rope_t, headmask, ident_in, pairmask,
               router, w1, w2, out):
    ctx = ExitStack()
    with ctx:
        def sb(name, shape, dt=F32):
            return ctx.enter_context(nc.sbuf_tensor(name, shape, dt))

        def sem(name):
            return ctx.enter_context(nc.semaphore(name))

        x_in = sb("x_in", [P, CHUNKS, P])
        x_res = sb("x_res", [P, CHUNKS, P])
        x_bias = sb("x_bias", [P, CHUNKS, P])
        x_mid = sb("x_mid", [P, CHUNKS, P])
        x_sum = sb("x_sum", [P, CHUNKS, P])
        x_nrm = sb("x_nrm", [P, CHUNKS, P])
        xnT = sb("xnT", [P, TOKENS])
        oT = xnT
        qT = sb("qT", [P, TOKENS])
        kE = sb("kE", [P, 2, TOKENS])
        kR = sb("kR", [P, 2, BANK])
        rope1 = sb("rope1", [P, 4, BANK])
        rope2 = sb("rope2", [P, 4, BANK])
        v_s = sb("v_s", [P, 32, PAIRS, 2 * VW])
        v_t = sb("v_t", [P, 32, PAIRS, 4 * VW])
        prob = sb("prob", [P, 2, PAIRS, 4, P])
        probT = sb("probT", [P, 2, 4, PAIRS, P])
        top = sb("top", [P, 2, 4 * BANK // 32])
        den = sb("den", [P, 2, 16])
        o_nrm = sb("o_nrm", [P, 8, 2 * P])
        ws = sb("ws", [P, WCOLS])
        wt = sb("wt", [P, WCOLS])
        vec = sb("vec", [P, 2, 4, P])
        b_both = sb("b_both", [P, P])
        cs_s = sb("cs_s", [P, 2, PATCH])
        cs_t = sb("cs_t", [P, 2, TIME])
        hmask = sb("hmask", [P, 2])
        ident = sb("ident", [P, P])
        pmask = sb("pmask", [2, P + BANK], BF16)
        stats = sb("stats", [P, HC, 6])
        mv = sb("mv", [P, 4, HC, 2])
        veps = sb("veps", [P, 4, HC])
        rstd = sb("rstd", [P, 4, HC])
        mhalf = sb("mhalf", [P, HC])
        rt = sb("rt", [P, EXPERTS])
        w1_sb = qT[:, 0:2 * FF].rearrange("p (s n) -> p s n", s=2)
        w2_sb = qT[:, 2 * FF:4 * FF].rearrange("p (s c n) -> p s c n", s=2, c=FC)
        hid = kE[:, :, :].rearrange("p s (c n) -> p s c n", c=FC)
        gate = sb("gate", [P, CHUNKS, 2, EXPERTS // 2])
        lg = sb("lg", [P, CHUNKS, EXPERTS])
        lmax = sb("lmax", [P, CHUNKS])
        lsum = sb("lsum", [P, CHUNKS])
        prb = sb("prb", [P, CHUNKS, EXPERTS])
        above = rope1[:, 0:2, :].rearrange("p a b -> p (a b)").rearrange("p (c e f) -> p c e f", c=CHUNKS, e=EXPERTS)
        ties = rope2[:, 0:2, :].rearrange("p a b -> p (a b)").rearrange("p (c e f) -> p c e f", c=CHUNKS, e=EXPERTS)
        before = sb("before", [P, EXPERTS, EXPERTS])
        rank = sb("rank", [P, CHUNKS, EXPERTS])

        score = ctx.enter_context(nc.psum_tensor("score", [P, 4, BANK], F32))
        turn = ctx.enter_context(nc.psum_tensor("turn", [P, 2, BANK], F32))
        small = ctx.enter_context(nc.psum_tensor("small", [P, 2, BANK], F32))

        loaded = sem("loaded")
        x_loaded = [sem(f"x_loaded{i}") for i in range(BATCH)]
        ready = sem("ready")
        stat_done = sem("stat_done")
        var_ready = sem("var_ready")
        rstd_ready = sem("rstd_ready")
        nrm_ready = sem("nrm_ready")
        turn_full = sem("turn_full")
        turn_free = [sem(f"turn_free{i}") for i in range(2)]
        small_full = sem("small_full")
        small_free = [sem(f"small_free{i}") for i in range(2)]
        proj_full = sem("proj_full")
        proj_free = sem("proj_free")
        rope_sum = sem("rope_sum")
        key_ready = sem("key_ready")
        score_full = sem("score_full")
        top_ready = sem("top_ready")
        score_free = sem("score_free")
        prob_ready = sem("prob_ready")
        den_ready = sem("den_ready")
        bias_ready = sem("bias_ready")
        both_ready = sem("both_ready")
        mid_ready = sem("mid_ready")
        fin_step = sem("fin_step")
        res_ready = sem("res_ready")
        add_ready = sem("add_ready")
        wt_loaded = sem("wt_loaded")
        vec_loaded = [sem(f"vec_loaded{i}") for i in range(2)]
        ws_loaded = sem("ws_loaded")
        route = sem("route")
        lg_ready = sem("lg_ready")
        lg_sub = sem("lg_sub")
        lg_exp = sem("lg_exp")
        w_loaded = [sem(f"w_loaded{i}") for i in range(2)]
        h_full = sem("h_full")
        h_free = sem("h_free")
        y_full = sem("y_full")
        y_free = sem("y_free")
        stored = sem("stored")
        arrived = sem("arrived")
        go = sem("go")
        left = sem("left")

        EXPERT_SEMS = [*w_loaded, h_full, h_free, y_full, y_free]

        def turn_end(eng):
            eng.drain().then_inc(arrived, 1)
            eng.wait_ge(go, 1)
            eng.drain().then_inc(left, 1)

        def turn_clear(sp, sems, engines):
            sp.wait_ge(arrived, engines)
            sp.drain()
            for s in (*sems, arrived):
                sp.sem_clear(s)
            sp.drain().then_inc(go, 1)
            sp.wait_ge(left, engines)
            sp.drain()
            sp.sem_clear(go)
            sp.sem_clear(left)
            sp.drain()

        def wait_read(eng, frees, use):
            eng.wait_ge(frees[use % 2], use // 2 + 1)

        def half_of(t, half):
            return t[:, half * HC:(half + 1) * HC, :]

        def flat(ap):
            return ap.rearrange("p c n -> p (c n)")

        block = ctx.enter_context(nc.Block())

        @block.sync
        def _(sp):
            for half in range(BATCH):
                sp.dma_start(half_of(x_in, half), half_of(x, half)).then_inc(x_loaded[half], 16)
            for dst, src in ((ws[:, :], w_s[0]), (ident[:, :], ident_in), (cs_s[:, :, :], rope_s),
                             (cs_t[:, :, :], rope_t), (hmask[:, :], headmask), (pmask[:, :], pairmask),
                             (rt[:, :], router)):
                sp.dma_start(dst, src).then_inc(loaded, 16)
            for n in range(DEPTH):
                if n >= 2:
                    sp.wait_ge(res_ready, 2 + 2 * (n - 1))
                sp.dma_start(vec[:, n % 2, :, :], vec_in[n:n + 1].broadcast_to([P, 4, P])).then_inc(vec_loaded[n % 2], 16)
                if n:
                    sp.wait_ge(small_full, STEPS["out", n - 1, T, 1, 0].smalls + 2)
                sp.dma_start(wt[:, :], w_t[n]).then_inc(wt_loaded, 16)
                if n + 1 < DEPTH:
                    sp.wait_ge(small_full, STEPS["out", n, S, 1, 0].smalls + 2)
                    sp.dma_start(ws[:, :], w_s[n + 1]).then_inc(ws_loaded, 16)
            sp.wait_ge(score_full, STEPS["score", DEPTH - 1, T, 1, 0].scores + 1)
            with sp.Fori(0, EXPERTS // 2) as pair:
                for s in range(2):
                    sp.dma_start(w1_sb[:, s, :], w1.rearrange("(q s) p n -> q s p n", s=2)[bass.ds(pair, 1), s]
                                 .rearrange("o p n -> p (o n)")).then_inc(w_loaded[s], 16)
                    sp.dma_start(w2_sb[:, s, :, :], w2.rearrange("(q s) p c n -> q s p c n", s=2)[bass.ds(pair, 1), s]
                                 .rearrange("o p c n -> p (o c) n")).then_inc(w_loaded[s], 16)
                for s in range(2):
                    sp.wait_ge(w_loaded[s], 32)
                turn_clear(sp, EXPERT_SEMS, 3)
            sp.dma_start(out, x_in[:, :, :]).then_inc(stored, 16)
            sp.wait_ge(stored, 16)

        @block.gpsimd
        def _(pool):
            nc.gpsimd.memset(mhalf[:, :], -0.5).then_inc(ready, 1)
            nc.gpsimd.memset(v_s[:, :, :, :], 0.0).then_inc(ready, 1)
            nc.gpsimd.memset(v_t[:, :, :, :], 0.0).then_inc(ready, 1)
            pool.wait_ge(ready, 1)
            for q in PLAN:
                if q.step == "stats":
                    pool.wait_ge(var_ready, q.nth + 1)
                    nc.gpsimd.tensor_tensor(rstd[:, q.nth % 4, :], veps[:, q.nth % 4, :], mhalf[:, :],
                                            ALU.pow).then_inc(rstd_ready, 1)
                elif q.step == "project":
                    for t in range(2):
                        tile = q.proj // 4 + t
                        cols = slice(q.half * HT + t * BANK, q.half * HT + (t + 1) * BANK)
                        pool.wait_ge(proj_free, 4 * tile + 2)
                        nc.gpsimd.tensor_tensor(qT[:, cols], rope1[:, (2 * tile) % 4, :], rope2[:, (2 * tile) % 4, :],
                                                ALU.add).then_inc(rope_sum, 1)
                        pool.wait_ge(proj_free, 4 * tile + 4)
                        if tile >= 2:
                            pool.wait_ge(key_ready, tile - 1)
                        nc.gpsimd.tensor_tensor(kR[:, tile % 2, :], rope1[:, (2 * tile + 1) % 4, :],
                                                rope2[:, (2 * tile + 1) % 4, :], ALU.add).then_inc(rope_sum, 1)
                elif q.step == "bias":
                    n = q.layer
                    if q.kind == S:
                        pool.wait_ge(vec_loaded[n % 2], 16 * (n // 2 + 1))
                        if q.half == 0:
                            nc.gpsimd.tensor_tensor(b_both[:, :], vec[:, n % 2, 0, :], vec[:, n % 2, 1, :],
                                                    ALU.add).then_inc(both_ready, 1)
                        pool.wait_ge(res_ready, 2 * n + q.half + 1)
                    else:
                        pool.wait_ge(mid_ready, 2 * (2 * n + q.half + 1))
                    row = 0 if q.kind == S else 3
                    nc.gpsimd.tensor_tensor(half_of(x_bias, q.half), half_of(x_res, q.half),
                                            vec[:, n % 2, row:row + 1, :].broadcast_to([P, HC, P]),
                                            ALU.add).then_inc(bias_ready, 1)

        @block.scalar
        def _(act):
            act.wait_ge(loaded, 16 * 7)
            act.wait_ge(ready, 9)
            for q in PLAN:
                if q.step == "turn":
                    if q.kind == T:
                        act.wait_ge(wt_loaded, 16 * (q.layer + 1))
                    elif q.kind == S and q.layer:
                        act.wait_ge(ws_loaded, 16 * q.layer)
                    for t in range(2):
                        u = q.turns + t
                        act.wait_ge(turn_full, u + 1)
                        src = turn[:, u % 2, :]
                        dst = xnT[:, q.half * HT + t * BANK:q.half * HT + (t + 1) * BANK]
                        if q.kind == E:
                            nc.scalar.activation(dst, src, ACT.Copy).then_inc(turn_free[u % 2], 1)
                            continue
                        w = ws if q.kind == S else wt
                        if q.kind == T:
                            src = src.rearrange("d (t p) -> d p t", p=PATCH)
                            dst = xnT[:, q.half * HT:(q.half + 1) * HT].rearrange("d (p t) -> d p t", t=TIME)[
                                :, :, t * 8:(t + 1) * 8]
                        nc.scalar.activation(dst, src, ACT.Identity, bias=w[:, BETA:BETA + 1],
                                             scale=w[:, GAMMA:GAMMA + 1]).then_inc(turn_free[u % 2], 1)
                elif q.step == "values":
                    br = BRANCH[q.kind]
                    v = v_s if q.kind == S else v_t
                    for t in range(2):
                        u = q.smalls + t
                        act.wait_ge(small_full, u + 1)
                        b0 = q.half * 16 + t * 8
                        for i in range(br.parts):
                            rows = slice(i * br.block, (i + 1) * br.block)
                            src = small[rows, u % 2, :].rearrange("p (u g d) -> p u g d", u=8, d=DH)
                            last = nc.scalar.activation(v[rows, b0:b0 + 8, :, i * VW:i * VW + DH], src, ACT.Copy)
                        last.then_inc(small_free[u % 2], 1)
                elif q.step == "project":
                    for t in range(2):
                        tile = q.proj // 4 + t
                        cols = slice(q.half * HT + t * BANK, q.half * HT + (t + 1) * BANK)
                        act.wait_ge(rope_sum, 2 * tile + 2)
                        for e in range(2):
                            last = nc.scalar.activation(kE[:, e, cols], kR[:, tile % 2, :], ACT.Copy, scale=hmask[:, e:e + 1])
                        last.then_inc(key_ready, 1)
                elif q.step == "less":
                    i = STEPS["score", q.layer, q.kind, q.half, q.group].scores
                    for h in range(2):
                        act.wait_ge(score_free, 2 * i + h + 1)
                        p = prob[:, i % 2, :, 2 * h:2 * h + 2, :].rearrange("p g k n -> p g (k n)")
                        nc.scalar.activation(p, p, ACT.Exp, scale=SCALE).then_inc(prob_ready, 1)
                elif q.step in ("head", "mix"):
                    for k in range(2):
                        u = q.turns + k
                        act.wait_ge(turn_full, u + 1)
                        nc.scalar.activation(flat(probT[:, q.nth % 2, k + 2 * (q.step == "mix"), :, :]), turn[:, u % 2, :],
                                             ACT.Copy).then_inc(turn_free[u % 2], 1)
                elif q.step == "out":
                    for t in range(2):
                        u = q.turns + t
                        act.wait_ge(turn_full, u + 1)
                        src = turn[:, u % 2, :]
                        dst = oT[:, q.half * HT + t * BANK:q.half * HT + (t + 1) * BANK]
                        if q.kind == T:
                            src = src.rearrange("d (p t) -> d t p", t=TIME)
                            dst = oT[:, q.half * HT:(q.half + 1) * HT].rearrange("d (t p) -> d t p", p=PATCH)[
                                :, :, t * 32:(t + 1) * 32]
                        nc.scalar.activation(dst, src, ACT.Copy).then_inc(turn_free[u % 2], 1)

            act.wait_ge(lg_sub, 1)
            nc.scalar.activation(prb[:, :, :], lg[:, :, :], ACT.Exp).then_inc(lg_exp, 1)

            with act.Fori(0, EXPERTS // 2):
                for n in range(8):
                    if n >= 2:
                        act.wait_ge(y_full, n - 1)
                    for c in range(FC):
                        act.wait_ge(h_full, n * FC + c + 1)
                        nc.scalar.activation(hid[:, n % 2, c, :], score[:, c, :], ACT.Gelu).then_inc(h_free, 1)
                turn_end(act)

        @block.tensor
        def _(pe):
            pe.wait_ge(loaded, 16 * 7)

            def turned(srcs, u):
                if u >= 2:
                    wait_read(pe, turn_free, u - 2)
                for j, src in enumerate(srcs):
                    last = nc.tensor.transpose(turn[:, u % 2, j * P:(j + 1) * P], src, ident[:, :])
                last.then_inc(turn_full, 1)

            def small_bank(u):
                if u >= 2:
                    wait_read(pe, small_free, u - 2)
                return small[:, u % 2, :]

            for q in PLAN:
                br = BRANCH.get(q.kind)
                w = ws if q.kind == S else wt
                n = br.block if br else 0
                if q.step == "turn":
                    normal = STEPS["normal", q.layer, q.kind, q.half, 0]
                    for t in range(2):
                        pe.wait_ge(nrm_ready, 2 * normal.nth + t + 1)
                        c0 = q.half * HC + 4 * t
                        turned([x_nrm[:, c, :] for c in range(c0, c0 + 4)], q.turns + t)
                elif q.step == "values":
                    for t in range(2):
                        bank = small_bank(q.smalls + t)
                        for v in range(8):
                            b = q.half * 16 + t * 8 + v
                            for i in range(br.parts):
                                if q.kind == S:
                                    tok = b * n
                                else:
                                    tok = (2 * (b // 4) + i // 2) * P + (b % 4) * n
                                h = i % 2
                                last = nc.tensor.matmul(bank[i * n:(i + 1) * n, v * 64:(v + 1) * 64], xnT[:, tok:tok + n],
                                                        w[:, WV + 64 * h:WV + 64 * h + 64], start=True, stop=True)
                        last.then_inc(small_full, 1)
                elif q.step == "project":
                    if q.scores:
                        pe.wait_ge(score_free, 2 * q.scores)
                    turn_step = STEPS["turn", q.layer, q.kind, q.half, 0]
                    for t in range(2):
                        wait_read(pe, turn_free, turn_step.turns + t)
                    for t in range(2):
                        cols = xnT[:, q.half * HT + t * BANK:q.half * HT + (t + 1) * BANK]
                        for j, off in enumerate((WQ, WQS, WK, WKS)):
                            i = q.proj + 4 * t + j
                            if i >= 4:
                                pe.wait_ge(proj_free, i - 3)
                            nc.tensor.matmul(score[:, j, :], w[:, off:off + P], cols, start=True,
                                             stop=True).then_inc(proj_full, 1)
                elif q.step == "score":
                    proj = STEPS["project", q.layer, q.kind, q.half, 0]
                    pe.wait_ge(rope_sum, proj.proj // 2 + 4)
                    pe.wait_ge(key_ready, proj.proj // 4 + 2)
                    pe.wait_ge(proj_free, q.proj)
                    if q.scores:
                        pe.wait_ge(score_free, 2 * q.scores)
                    if q.kind == T:
                        for g in range(PAIRS):
                            nc.tensor.matmul(score[:, g, :], pmask[:, 0:P], pmask[:, P:P + BANK], start=True, stop=False,
                                             skip_group_check=True)
                    for c in range(br.group_chunks):
                        chunk = q.half * HC + q.group * br.group_chunks + c
                        for b in range(br.blocks):
                            tok = chunk * P + b * n
                            for g in range(PAIRS):
                                rows = slice(32 * g, 32 * g + 32)
                                last = nc.tensor.matmul(
                                    score[b * n:(b + 1) * n, g, c * 2 * n:(c + 1) * 2 * n], qT[rows, tok:tok + n],
                                    kE[rows, :, tok:tok + n], start=q.kind == S, stop=True,
                                    skip_group_check=q.kind == T, tile_position=(32 * g, b * n))
                    last.then_inc(score_full, 1)
                elif q.step == "head":
                    i = STEPS["score", q.layer, q.kind, q.half, q.group].scores
                    pe.wait_ge(prob_ready, 2 * i + 1)
                    for k in range(2):
                        turned([prob[:, i % 2, g, k, :] for g in range(PAIRS)], q.turns + k)
                elif q.step == "mix":
                    i = STEPS["score", q.layer, q.kind, q.half, q.group].scores
                    head = STEPS["head", q.layer, q.kind, q.half, q.group]
                    values = STEPS["values", q.layer, q.kind, q.half, 0]
                    v = v_s if q.kind == S else v_t

                    def weighted(k):
                        wait_read(pe, turn_free, head.turns + k if k < 2 else q.turns + k - 2)
                        if q.kind == S:
                            unit, first, full = q.smalls + k // 2, k % 2 == 0, k % 2 == 1
                            blk0 = (q.half * HC + q.group * 4 + k) * 2
                        else:
                            unit, first, full = q.smalls + k, True, True
                            blk0 = q.half * 16 + k * 4
                        bank = small_bank(unit) if first else small[:, unit % 2, :]
                        if k == 0:
                            wait_read(pe, small_free, values.smalls)
                            wait_read(pe, small_free, values.smalls + 1)
                        cols = bank[:, 0:16 * VW].rearrange("p (c g w) -> p c g w", c=2, g=PAIRS)
                        if q.kind == S:
                            cols = cols[:, k % 2:k % 2 + 1, :, :]
                        for b in range(br.blocks):
                            for g in range(PAIRS):
                                last = nc.tensor.matmul(
                                    cols[b * n:(b + 1) * n, :, g, :],
                                    probT[:, q.nth % 2, k, g, b * n:(b + 1) * n], v[:, blk0 + b, g, :], start=True, stop=True)
                        if full:
                            last.then_inc(small_full, 1)

                    weighted(0)
                    pe.wait_ge(prob_ready, 2 * i + 2)
                    turned([prob[:, i % 2, g, 2, :] for g in range(PAIRS)], q.turns)
                    weighted(1)
                    turned([prob[:, i % 2, g, 3, :] for g in range(PAIRS)], q.turns + 1)
                    weighted(2)
                    weighted(3)
                elif q.step == "out":
                    mix = STEPS["mix", q.layer, q.kind, q.half, br.groups - 1]
                    units = 2 if q.kind == S else 4
                    for z in range(units - 2, units):
                        wait_read(pe, small_free, mix.smalls + z)
                    for t in range(2):
                        turned([o_nrm[:, q.half * 4 + c // 2, (c % 2) * P:(c % 2 + 1) * P] for c in range(4 * t, 4 * t + 4)],
                               q.turns + t)
                    for t in range(2):
                        if q.kind == T:
                            wait_read(pe, turn_free, q.turns + 1)
                        wait_read(pe, turn_free, q.turns + t)
                        bank = small_bank(q.smalls + t)
                        for j in range(4):
                            c = q.half * HC + 4 * t + j
                            last = nc.tensor.matmul(bank[:, j * P:(j + 1) * P], oT[:, c * P:(c + 1) * P], w[:, WO:WO + P],
                                                    start=True, stop=True)
                        last.then_inc(small_full, 1)

            def wait_features(half):
                q = STEPS["turn", DEPTH - 1, E, half, 0]
                wait_read(pe, turn_free, q.turns)
                wait_read(pe, turn_free, q.turns + 1)

            wait_features(0)
            wait_features(1)
            for z in range(2):
                wait_read(pe, small_free, STEPS["out", DEPTH - 1, T, 1, 0].smalls + z)
            for c in range(CHUNKS):
                last = nc.tensor.matmul(small[:, 0, c * EXPERTS:(c + 1) * EXPERTS], xnT[:, c * P:(c + 1) * P], rt[:, :],
                                        start=True, stop=True)
            last.then_inc(lg_ready, 1)
            pe.wait_ge(score_free, 2 * (STEPS["score", DEPTH - 1, T, 1, 0].scores + 1))
            pe.wait_ge(lg_sub, 1)

            with pe.Fori(0, EXPERTS // 2):
                def second(n):
                    if n >= 2:
                        pe.wait_ge(y_free, n - 1)
                    for j in range(4):
                        for c in range(FC):
                            if j == 0:
                                pe.wait_ge(h_free, n * FC + c + 1)
                            last = nc.tensor.matmul(small[:, n % 2, j * P:(j + 1) * P], hid[:, n % 2, c, j * P:(j + 1) * P],
                                                    w2_sb[:, n // 4, c, :], start=c == 0, stop=c == FC - 1)
                    last.then_inc(y_full, 1)

                for n in range(8):
                    pe.wait_ge(w_loaded[n // 4], 32)
                    for c in range(FC):
                        if n >= 1:
                            pe.wait_ge(h_free, (n - 1) * FC + c + 1)
                        nc.tensor.matmul(score[:, c, :], w1_sb[:, n // 4, c * P:(c + 1) * P],
                                         xnT[:, (n % 4) * BANK:(n % 4 + 1) * BANK], start=True, stop=True).then_inc(h_full, 1)
                    if n >= 1:
                        second(n - 1)
                second(7)
                turn_end(pe)

        @block.vector
        def _(dve):
            dve.wait_ge(ready, 3)
            for br, v in ((SPATIAL, v_s), (TEMPORAL, v_t)):
                for i in range(br.parts):
                    nc.vector.memset(v[i * br.block:(i + 1) * br.block, :, :, i * VW + DH:(i + 1) * VW], 1.0).then_inc(ready, 1)
            dve.wait_ge(loaded, 16 * 7)
            moments = 0
            finals = 0
            for q in PLAN:
                if q.step == "stats":
                    if q.kind == C:
                        dve.wait_ge(x_loaded[q.half], 16)
                    if q.kind == E:
                        nc.vector.tensor_tensor(half_of(x_in, q.half), half_of(x_in, q.half), half_of(x_res, q.half),
                                                ALU.add).then_inc(add_ready, 1)
                        dve.wait_ge(add_ready, q.half + 1)
                    src = {C: x_in, S: x_res, T: x_mid, F: x_sum, E: x_in}[q.kind]
                    slot = q.nth % 4
                    for c in range(HC):
                        nc.vector.bn_stats(stats[:, c, :], src[:, q.half * HC + c, :]).then_inc(stat_done, 1)
                    moments += HC
                    dve.wait_ge(stat_done, moments)
                    for c in range(HC):
                        nc.vector.bn_aggr(mv[:, slot, c, :], stats[:, c, :]).then_inc(stat_done, 1)
                    moments += HC
                    dve.wait_ge(stat_done, moments)
                    eps = CONV_EPS if q.kind == C else NORM_EPS
                    nc.vector.tensor_scalar(veps[:, slot, :], mv[:, slot, :, 1], eps, None, ALU.add).then_inc(var_ready, 1)
                elif q.step == "normal":
                    stat = STEPS["stats", q.layer, q.kind, q.half, 0]
                    slot = stat.nth % 4
                    src = {C: x_in, S: x_res, T: x_mid, F: x_sum, E: x_in}[q.kind]
                    dst = {C: x_res, F: x_nrm}.get(q.kind, x_nrm)
                    dve.wait_ge(rstd_ready, stat.nth + 1)
                    for c in range(HC):
                        k = q.half * HC + c
                        last = nc.vector.tensor_scalar(dst[:, k, :], src[:, k, :], mv[:, slot, c, 0:1],
                                                       rstd[:, slot, c:c + 1], ALU.subtract, ALU.mult)
                        if c % 4 == 3:
                            last.then_inc(nrm_ready, 1)
                    if q.kind == C:
                        dve.wait_ge(nrm_ready, 2 * q.nth + 2)
                        dve.sem_inc(res_ready, 1)
                    if q.kind == F:
                        dve.wait_ge(nrm_ready, 2 * q.nth + 2)
                        scaled = half_of(x_nrm, q.half)
                        nc.vector.tensor_tensor(scaled, scaled, vec[:, q.layer % 2, 2:3, :].broadcast_to([P, HC, P]),
                                                ALU.mult).then_inc(fin_step, 1)
                        finals += 1
                        dve.wait_ge(fin_step, finals)
                        dve.wait_ge(bias_ready, STEPS["bias", q.layer, F, q.half, 0].nth + 1)
                        nc.vector.tensor_tensor(half_of(x_res, q.half), scaled, half_of(x_bias, q.half),
                                                ALU.add).then_inc(res_ready, 1)
                        dve.wait_ge(res_ready, 2 + 2 * q.layer + q.half + 1)
                elif q.step == "project":
                    table, length = (cs_s, PATCH) if q.kind == S else (cs_t, TIME)
                    for j in range(8):
                        i = q.proj + j
                        r = i // 2
                        dst = (rope1 if i % 2 == 0 else rope2)[:, r % 4, :]
                        if r >= 4:
                            dve.wait_ge(rope_sum, r - 3)
                        dve.wait_ge(proj_full, i + 1)
                        nc.vector.tensor_tensor(
                            dst.rearrange("p (s n) -> p s n", n=length),
                            score[:, i % 4, :].rearrange("p (s n) -> p s n", n=length),
                            table[:, i % 2, None, :].broadcast_to([P, BANK // length, length]), ALU.mult).then_inc(proj_free, 1)
                elif q.step == "most":
                    i = STEPS["score", q.layer, q.kind, q.half, q.group].scores
                    block_len = BRANCH[q.kind].block
                    rows = 4 * BANK // block_len
                    dve.wait_ge(score_full, i + 1)
                    nc.vector.tensor_reduce(top[:, i % 2, 0:rows],
                                            score[:, :, :].rearrange("p g (r n) -> p (g r) n", n=block_len),
                                            AX_X, ALU.max).then_inc(top_ready, 1)
                elif q.step == "less":
                    i = STEPS["score", q.layer, q.kind, q.half, q.group].scores
                    block_len = BRANCH[q.kind].block
                    rows = 4 * BANK // block_len
                    dve.wait_ge(top_ready, i + 1)
                    per = BANK // block_len
                    for h in range(2):
                        tops = top[:, i % 2, 0:rows].rearrange("p (g r) -> p g r", g=PAIRS)[:, :, h * per // 2:(h + 1) * per // 2]
                        nc.vector.tensor_tensor(
                            prob[:, i % 2, :, 2 * h:2 * h + 2, :].rearrange("p g k (r n) -> p g (k r) n", n=block_len),
                            score[:, :, h * 256:(h + 1) * 256].rearrange("p g (r n) -> p g r n", n=block_len),
                            tops[:, :, :, None].broadcast_to([P, PAIRS, per // 2, block_len]),
                            ALU.subtract).then_inc(score_free, 1)
                elif q.step == "divide":
                    mix = STEPS["mix", q.layer, q.kind, q.half, q.group if q.kind == S else 0]
                    first = mix.smalls + (0 if q.kind == S else 2 * q.group)
                    for z in range(2):
                        u = first + z
                        dve.wait_ge(small_full, u + 1)
                        src = small[:, u % 2, 0:16 * VW].rearrange("p (h d) -> p h d", d=VW)
                        nc.vector.reciprocal(den[:, u % 2, :], src[:, :, DH]).then_inc(den_ready, 1)
                        dve.wait_ge(den_ready, 2 * q.nth + z + 1)
                        nc.vector.tensor_tensor(o_nrm[:, q.half * 4 + q.group * 2 + z, :].rearrange("p (h d) -> p h d", d=DH),
                                                src[:, :, 0:DH], den[:, u % 2, :, None].broadcast_to([P, 16, DH]),
                                                ALU.mult).then_inc(small_free[u % 2], 1)
                elif q.step == "out" and q.kind == S:
                    dve.wait_ge(bias_ready, STEPS["bias", q.layer, S, q.half, 0].nth + 1)
                    dve.wait_ge(both_ready, q.layer + 1)
                    for t in range(2):
                        u = q.smalls + t
                        c0 = q.half * HC + 4 * t
                        dve.wait_ge(small_full, u + 1)
                        src = small[:, u % 2, :].rearrange("p (c n) -> p c n", n=P)
                        nc.vector.tensor_tensor(x_mid[:, c0:c0 + 4, :], src, x_bias[:, c0:c0 + 4, :], ALU.add).then_inc(mid_ready, 1)
                        nc.vector.tensor_tensor(x_sum[:, c0:c0 + 4, :], src, b_both[:, None, :].broadcast_to([P, 4, P]),
                                                ALU.add).then_inc(small_free[u % 2], 1)
                    dve.wait_ge(mid_ready, 2 * (2 * q.layer + q.half + 1))
                elif q.step == "out":
                    for t in range(2):
                        u = q.smalls + t
                        c0 = q.half * HC + 4 * t
                        dve.wait_ge(small_full, u + 1)
                        z = flat(x_sum[:, c0:c0 + 4, :])
                        nc.vector.tensor_tensor(z, small[:, u % 2, :], z, ALU.add).then_inc(small_free[u % 2], 1)
                    for t in range(2):
                        wait_read(dve, small_free, q.smalls + t)

            chain = [0]

            def link(ins):
                chain[0] += 1
                ins.then_inc(route, 1)
                dve.wait_ge(route, chain[0])

            link(nc.vector.memset(before[:, :, :], 0.0))
            for e in range(1, EXPERTS):
                last = nc.vector.memset(before[:, e, 0:e], 1.0)
                last.then_inc(route, 1)
                chain[0] += 1
            dve.wait_ge(route, chain[0])
            dve.wait_ge(lg_ready, 1)
            logits = small[:, 0, 0:CHUNKS * EXPERTS].rearrange("p (c e) -> p c e", e=EXPERTS)
            link(nc.vector.tensor_reduce(lmax[:, :], logits, AX_X, ALU.max))
            nc.vector.tensor_tensor(lg[:, :, :], logits, lmax[:, :, None].broadcast_to([P, CHUNKS, EXPERTS]),
                                    ALU.subtract).then_inc(lg_sub, 1)
            dve.wait_ge(lg_exp, 1)
            link(nc.vector.tensor_reduce(lsum[:, :], prb[:, :, :], AX_X, ALU.add))
            link(nc.vector.reciprocal(lmax[:, :], lsum[:, :]))
            link(nc.vector.tensor_tensor(lg[:, :, :], prb[:, :, :], lmax[:, :, None].broadcast_to([P, CHUNKS, EXPERTS]), ALU.mult))
            mine = lg[:, :, :, None].broadcast_to([P, CHUNKS, EXPERTS, EXPERTS])
            others = lg[:, :, None, :].broadcast_to([P, CHUNKS, EXPERTS, EXPERTS])
            link(nc.vector.tensor_tensor(above, others, mine, ALU.is_gt))
            link(nc.vector.tensor_tensor(ties, others, mine, ALU.is_equal))
            link(nc.vector.tensor_tensor(ties, ties, before[:, None, :, :].broadcast_to([P, CHUNKS, EXPERTS, EXPERTS]), ALU.mult))
            link(nc.vector.tensor_tensor(above, above, ties, ALU.add))
            link(nc.vector.tensor_reduce(rank[:, :, :], above, AX_X, ALU.add))
            link(nc.vector.tensor_scalar(rank[:, :, :], rank[:, :, :], 1.5, None, ALU.is_lt))
            link(nc.vector.tensor_tensor(gate[:, :, :, :].rearrange("p c s q -> p c q s"), lg[:, :, :].rearrange("p c (q s) -> p c q s", s=2),
                                         rank[:, :, :].rearrange("p c (q s) -> p c q s", s=2), ALU.mult))

            with dve.Fori(0, EXPERTS // 2) as pair:
                for n in range(8):
                    dve.wait_ge(y_full, n + 1)
                    for j in range(4):
                        c = (n % 4) * 4 + j
                        last = nc.vector.scalar_tensor_tensor(
                            out=x_in[:, c, :], in0=small[:, n % 2, j * P:(j + 1) * P],
                            scalar=gate[:, c, n // 4, bass.ds(pair, 1)], in1=x_in[:, c, :], op0=ALU.mult, op1=ALU.add)
                    last.then_inc(y_free, 1)
                turn_end(dve)


def rope_table(length):
    import numpy as np
    freq = (1.0 / np.float32(10000.0) ** (np.arange(0, DH, 2, dtype=np.float32) / np.float32(DH))).astype(np.float32)
    angle = (np.arange(length, dtype=np.float32)[:, None] * freq[None, :]).astype(np.float32)
    angle = np.repeat(angle, 2, axis=-1).T
    sign = np.where(np.arange(DH) % 2 == 0, -1.0, 1.0)[:, None]
    cos = np.tile(np.cos(angle.astype(np.float64)), (HEADS, 1))
    sin = np.tile(np.sin(angle.astype(np.float64)) * sign, (HEADS, 1))
    return np.ascontiguousarray(np.stack([cos, sin], axis=1).astype(np.float32))


def kernel(**inputs):
    import numpy as np
    import concourse.bacc as bacc
    from concourse.bass_utils import run_bass_kernel_spmd

    a = {k: np.asarray(v) for k, v in inputs.items()}

    def packed(tag):
        qkv = a[f"L0_conv_w_qkv_{tag}"]
        q, k, v = qkv[:, :, 0:P], qkv[:, :, P:2 * P], qkv[:, :, 2 * P:3 * P]
        swap = np.arange(P) ^ 1
        v = v.reshape(DEPTH, P, PAIRS, 2, DH).transpose(0, 1, 3, 2, 4).reshape(DEPTH, P, P)
        w = np.concatenate([q, k, q[:, :, swap], k[:, :, swap], v, a[f"L0_conv_w_out_{tag}"],
                            a[f"L0_conv_ln_{tag}_g"][:, :, None], a[f"L0_conv_ln_{tag}_b"][:, :, None]], axis=2)
        return np.ascontiguousarray(w)

    parity = np.zeros((2, P + BANK), np.float32)
    for r in range(2):
        parity[r, 0:P] = (np.arange(P) // TIME) % 2 == r
        parity[r, P:] = np.where((np.arange(BANK) // TIME) % 2 == r, 0.0, -1e30)
    import ml_dtypes
    arrays = {
        "x": np.ascontiguousarray(a["x"].reshape(CHUNKS, P, P).transpose(1, 0, 2)),
        "w_s": packed("s"),
        "w_t": packed("t"),
        "vec_in": np.ascontiguousarray(np.stack([a["L0_conv_b_out_s"], a["L0_conv_b_out_t"], a["L0_conv_ln_f_g"],
                                                 a["L0_conv_ln_f_b"]], axis=1)),
        "rope_s": rope_table(PATCH),
        "rope_t": rope_table(TIME),
        "headmask": np.ascontiguousarray(np.stack([(np.arange(P) // DH) % 2 == e for e in range(2)], axis=1).astype(np.float32)),
        "ident": np.eye(P, dtype=np.float32),
        "pairmask": parity.astype(ml_dtypes.bfloat16),
        "router": np.ascontiguousarray(a["L0_ffn_Wr"]),
        "w1": np.ascontiguousarray(a["L0_ffn_W1"]),
        "w2": np.ascontiguousarray(a["L0_ffn_W2"].reshape(EXPERTS, FC, P, P).transpose(0, 2, 1, 3)),
    }
    nc = bacc.Bacc("TRN2", target_bir_lowering=False, num_devices=1)
    args = [nc.dram_tensor(f"in_{k}", v.shape, mybir.dt.from_np(v.dtype), kind="ExternalInput").ap()
            for k, v in arrays.items()]
    out = nc.dram_tensor("out_x", (P, CHUNKS, P), F32, kind="ExternalOutput").ap()
    metaformer(nc, *args, out)
    r = run_bass_kernel_spmd(nc, [{f"in_{k}": v for k, v in arrays.items()}], core_ids=[0])
    got = r.results[0]["out_x"]
    return np.ascontiguousarray(got.transpose(1, 0, 2)).reshape(BATCH, TIME, PATCH, P)
```

```python
from contextlib import ExitStack

from concourse import mybir

ALU = mybir.AluOpType
ACT = mybir.ActivationFunctionType
F32 = mybir.dt.float32
BF16 = mybir.dt.bfloat16
F32R = mybir.dt.float32r
AX_X = mybir.AxisListType.X

P = 128
BATCH, TIME, PATCH = 2, 16, 64
TOKENS = BATCH * TIME * PATCH
CHUNKS = TOKENS // P
HC = CHUNKS // BATCH
HT = TOKENS // BATCH
DEPTH, HEADS, DH = 4, 8, 16
PAIRS = HEADS // 2
BANK = 512
VW = DH + 1
EXPERTS, FF = 8, 512
FC = FF // P
ROUTE_LINKS = 4 + BATCH * 8
CONV_EPS, NORM_EPS = 1e-6, 1e-5
SCALE = DH ** -0.5
SWAP = [i ^ 1 for i in range(32)]

WQ, WK, WV, WO, GAMMA, BETA, WCOLS = 0, 128, 256, 384, 512, 513, 514


class Branch:

    def __init__(self, name, block, groups):
        self.name = name
        self.block = block
        self.blocks = P // block
        self.parts = P // block
        self.groups = groups
        self.group_chunks = HC // groups


SPATIAL = Branch("s", 64, 2)
TEMPORAL = Branch("t", 32, 1)

S, T, C, F, E = "s", "t", "c", "f", "e"


def layer_steps(n):
    p, m = n - 1, n + 1
    order = [
        ("bias", n, S, 0, 0), ("head", p, T, 1, 0), ("score", n, S, 0, 0), ("mix", p, T, 1, 0),
        ("soft", n, S, 0, 0), ("rest", n, S, 0, 0), ("divide", p, T, 1, 0), ("divide", p, T, 1, 1),
        ("out", p, T, 1, 0), ("stats", p, F, 1, 0), ("head", n, S, 0, 0), ("score", n, S, 0, 1),
        ("soft", n, S, 0, 1), ("mix", n, S, 0, 0), ("rest", n, S, 0, 1), ("divide", n, S, 0, 0),
        ("final", p, F, 1, 0), ("stats", n, S, 1, 0), ("head", n, S, 0, 1), ("mix", n, S, 0, 1),
        ("divide", n, S, 0, 1), ("normal", n, S, 1, 0), ("out", n, S, 0, 0), ("bias", n, S, 1, 0),
        ("stats", n, T, 0, 0), ("normal", n, T, 0, 0), ("turn", n, S, 1, 0), ("project", n, S, 1, 0),
        ("turn", n, T, 0, 0), ("project", n, T, 0, 0), ("part", n, S, 1, 0), ("values", n, S, 1, 0),
        ("values", n, T, 0, 0), ("score", n, S, 1, 0), ("soft", n, S, 1, 0), ("rest", n, S, 1, 0),
        ("head", n, S, 1, 0), ("part", n, T, 0, 0), ("score", n, S, 1, 1), ("soft", n, S, 1, 1),
        ("mix", n, S, 1, 0), ("rest", n, S, 1, 1), ("divide", n, S, 1, 0), ("head", n, S, 1, 1),
        ("score", n, T, 0, 0), ("mix", n, S, 1, 1), ("soft", n, T, 0, 0), ("rest", n, T, 0, 0),
        ("divide", n, S, 1, 1), ("out", n, S, 1, 0), ("stats", n, T, 1, 0), ("bias", n, F, 0, 0),
        ("normal", n, T, 1, 0), ("head", n, T, 0, 0), ("mix", n, T, 0, 0), ("divide", n, T, 0, 0),
        ("divide", n, T, 0, 1), ("turn", n, T, 1, 0), ("bias", n, F, 1, 0), ("project", n, T, 1, 0),
        ("out", n, T, 0, 0), ("stats", n, F, 0, 0), ("part", n, T, 1, 0), ("final", n, F, 0, 0),
        ("stats", m, S, 0, 0), ("values", n, T, 1, 0), ("score", n, T, 1, 0), ("soft", n, T, 1, 0),
        ("normal", m, S, 0, 0), ("turn", m, S, 0, 0), ("rest", n, T, 1, 0), ("project", m, S, 0, 0),
        ("part", m, S, 0, 0), ("values", m, S, 0, 0),
    ]
    return [step for step in order if 0 <= step[1] < DEPTH]


def all_steps():
    last = DEPTH - 1
    first_steps = [
        ("stats", 0, C, 0, 0), ("stats", 0, C, 1, 0), ("normal", 0, C, 0, 0), ("stats", 0, S, 0, 0),
        ("normal", 0, S, 0, 0), ("turn", 0, S, 0, 0), ("normal", 0, C, 1, 0), ("project", 0, S, 0, 0),
        ("part", 0, S, 0, 0), ("values", 0, S, 0, 0),
    ]
    last_steps = [
        ("stats", last, E, 0, 0), ("head", last, T, 1, 0), ("mix", last, T, 1, 0), ("divide", last, T, 1, 0),
        ("divide", last, T, 1, 1), ("normal", last, E, 0, 0), ("out", last, T, 1, 0), ("turn", last, E, 0, 0),
        ("stats", last, F, 1, 0), ("final", last, F, 1, 0), ("stats", last, E, 1, 0), ("normal", last, E, 1, 0),
        ("split", last, E, 0, 0), ("logits", last, E, 0, 0), ("turn", last, E, 1, 0), ("split", last, E, 1, 0),
        ("logits", last, E, 1, 0),
    ]
    return first_steps + [step for n in range(DEPTH) for step in layer_steps(n)] + last_steps


USES = {"project": (4, 0, 0, 0), "values": (0, 0, 0, 2), "score": (0, 1, 0, 0), "turn": (0, 0, 2, 0),
        "head": (0, 0, 2, 0), "out": (0, 0, 2, 2), "logits": (0, 0, 0, 1)}


class Step:

    def __init__(self, key, nth, used):
        self.step, self.layer, self.kind, self.half, self.group = key
        self.nth = nth
        self.proj, self.scores, self.turns, self.smalls = used


def numbered():
    used, seen, out = [0, 0, 0, 0], {}, {}
    for key in all_steps():
        step, kind = key[0], key[2]
        out[key] = Step(key, seen.get(step, 0), used)
        seen[step] = seen.get(step, 0) + 1
        takes = (0, 0, 2, 2 if kind == S else 4) if step == "mix" else USES.get(step, (0, 0, 0, 0))
        used = [a + b for a, b in zip(used, takes)]
    return out


STEPS = numbered()
PLAN = list(STEPS.values())
BRANCH = {S: SPATIAL, T: TEMPORAL}


def metaformer(nc, x, w_s, w_t, vec_in, rope_s, rope_t, headmask, ident_in, pairmask,
               router, w1, w2, out):
    ctx = ExitStack()
    with ctx:
        def sb(name, shape, dt=F32, until=ctx):
            return until.enter_context(nc.sbuf_tensor(name, shape, dt))

        def sem(name):
            return ctx.enter_context(nc.semaphore(name))

        x_in = sb("x_in", [P, CHUNKS, P])
        xnT = sb("xnT", [P, TOKENS])
        oT = xnT
        x_hi = sb("x_hi", [P, TOKENS], F32R)
        x_lo = sb("x_lo", [P, TOKENS], F32R)
        w_raw = sb("w_raw", [P, 2, FF])
        w_even = sb("w_even", [P, 2, 2, FF], F32R)
        ident = sb("ident", [P, P])
        rt = sb("rt", [P, EXPERTS])
        logit = sb("logit", [P, CHUNKS, EXPERTS])

        layers = ctx.enter_context(ExitStack())

        def lb(name, shape, dt=F32):
            return sb(name, shape, dt, layers)

        x_res = lb("x_res", [P, CHUNKS, P])
        x_bias = lb("x_bias", [P, CHUNKS, P])
        x_mid = lb("x_mid", [P, CHUNKS, P])
        x_sum = lb("x_sum", [P, CHUNKS, P])
        x_nrm = lb("x_nrm", [P, CHUNKS, P])
        qT = lb("qT", [P, TOKENS])
        kE = lb("kE", [P, 2, TOKENS])
        kR = lb("kR", [P, 2, BANK])
        rope1 = lb("rope1", [P, 4, BANK])
        rope2 = lb("rope2", [P, 4, BANK])
        v_s = lb("v_s", [P, 16, PAIRS, 2 * VW])
        v_t = lb("v_t", [P, 16, PAIRS, 4 * VW])
        prob = lb("prob", [P, 2, PAIRS, 4, P])
        probT = lb("probT", [P, 2, 4, PAIRS, P])
        top = lb("top", [P, 2, 2, 2 * BANK // 32])
        den = lb("den", [P, 2, 16])
        o_nrm = lb("o_nrm", [P, 4, 2 * P])
        ws = lb("ws", [P, WCOLS])
        wt = lb("wt", [P, WCOLS])
        vec = lb("vec", [P, 2, 4, P])
        b_both = lb("b_both", [P, P])
        cs_s = lb("cs_s", [P, 2, PATCH])
        cs_t = lb("cs_t", [P, 2, TIME])
        hmask = lb("hmask", [P, 2])
        pmask = lb("pmask", [2, P + BANK], BF16)
        stats = lb("stats", [P, HC, 6])
        mv = lb("mv", [P, 4, HC, 2])
        veps = lb("veps", [P, 4, HC])
        rstd = lb("rstd", [P, 4, HC])
        mhalf = lb("mhalf", [P, HC])

        score = ctx.enter_context(nc.psum_tensor("score", [P, 4, BANK], F32))
        turn = ctx.enter_context(nc.psum_tensor("turn", [P, 2, BANK], F32))
        small = ctx.enter_context(nc.psum_tensor("small", [P, 2, BANK], F32))

        loaded = sem("loaded")
        x_loaded = [sem(f"x_loaded{i}") for i in range(BATCH)]
        ready = sem("ready")
        stat_done = sem("stat_done")
        var_ready = sem("var_ready")
        rstd_ready = sem("rstd_ready")
        nrm_ready = sem("nrm_ready")
        turn_full = sem("turn_full")
        turn_free = [sem(f"turn_free{i}") for i in range(2)]
        small_full = sem("small_full")
        small_free = [sem(f"small_free{i}") for i in range(2)]
        proj_full = sem("proj_full")
        proj_free = sem("proj_free")
        swapped = sem("swapped")
        rope_done = sem("rope_done")
        rope_sum = sem("rope_sum")
        key_ready = sem("key_ready")
        score_full = sem("score_full")
        top_ready = sem("top_ready")
        score_free = sem("score_free")
        prob_ready = sem("prob_ready")
        den_ready = sem("den_ready")
        bias_ready = sem("bias_ready")
        both_ready = sem("both_ready")
        mid_ready = sem("mid_ready")
        fin_step = sem("fin_step")
        res_ready = sem("res_ready")
        add_ready = sem("add_ready")
        wt_loaded = sem("wt_loaded")
        vec_loaded = [sem(f"vec_loaded{i}") for i in range(2)]
        ws_loaded = sem("ws_loaded")
        route = sem("route")
        lg_sub = sem("lg_sub")
        lg_exp = sem("lg_exp")
        split_done = sem("split_done")
        raw_loaded = sem("raw_loaded")
        rounded = sem("rounded")
        w_split = sem("w_split")
        gates_turned = sem("gates_turned")
        gates_out = sem("gates_out")
        gates_kept = sem("gates_kept")
        gate_loaded = [sem(f"gate_loaded{e}") for e in range(EXPERTS)]
        first_gates = [sem(f"first_gates{t}") for t in range(TOKENS // BANK)]
        h_full = sem("h_full")
        h_ready = sem("h_ready")
        lo_ready = sem("lo_ready")
        y_full = sem("y_full")
        y_gated = sem("y_gated")
        y_added = sem("y_added")
        sum_turned = sem("sum_turned")
        out_ready = sem("out_ready")
        stored = sem("stored")

        def wait_read(eng, frees, use):
            eng.wait_ge(frees[use % 2], use // 2 + 1)

        def half_of(t, half):
            return t[:, half * HC:(half + 1) * HC, :]

        def flat(ap):
            return ap.rearrange("p c n -> p (c n)")

        def load_expert(sp, e):
            if e:
                sp.wait_ge(w_split, e)
            sp.dma_start(w_raw[:, 0, :], w1[e]).then_inc(raw_loaded, 16)
            sp.dma_start(w_raw[:, 1, :], w2[e].rearrange("p c n -> p (c n)")).then_inc(raw_loaded, 16)

        def split_expert(pool, e, dst):
            pool.wait_ge(raw_loaded, 32 * (e + 1))
            nc.gpsimd.tensor_copy(dst[:, 0], w_raw[:, :, :]).then_inc(rounded, 1)
            pool.wait_ge(rounded, e + 1)
            nc.gpsimd.tensor_tensor(dst[:, 1], w_raw[:, :, :], dst[:, 0].bitcast(F32), ALU.subtract).then_inc(w_split, 1)

        block = layers.enter_context(nc.Block())

        @block.sync
        def _(sp):
            for half in range(BATCH):
                sp.dma_start(half_of(x_in, half), half_of(x, half)).then_inc(x_loaded[half], 16)
            for dst, src in ((ws[:, :], w_s[0]), (ident[:, :], ident_in), (cs_s[:, :, :], rope_s),
                             (cs_t[:, :, :], rope_t), (hmask[:, :], headmask), (pmask[:, :], pairmask),
                             (rt[:, :], router)):
                sp.dma_start(dst, src).then_inc(loaded, 16)
            load_expert(sp, 0)
            for n in range(DEPTH):
                if n >= 2:
                    sp.wait_ge(res_ready, 2 + 2 * (n - 1))
                sp.dma_start(vec[:, n % 2, :, :], vec_in[n:n + 1].broadcast_to([P, 4, P])).then_inc(vec_loaded[n % 2], 16)
                if n:
                    sp.wait_ge(small_full, STEPS["out", n - 1, T, 1, 0].smalls + 2)
                sp.dma_start(wt[:, :], w_t[n]).then_inc(wt_loaded, 16)
                if n + 1 < DEPTH:
                    sp.wait_ge(small_full, STEPS["out", n, S, 1, 0].smalls + 2)
                    sp.dma_start(ws[:, :], w_s[n + 1]).then_inc(ws_loaded, 16)
        @block.gpsimd
        def _(pool):
            nc.gpsimd.memset(mhalf[:, :], -0.5).then_inc(ready, 1)
            nc.gpsimd.memset(v_s[:, :, :, :], 0.0).then_inc(ready, 1)
            nc.gpsimd.memset(v_t[:, :, :, :], 0.0).then_inc(ready, 1)
            pool.wait_ge(ready, 1)
            for q in PLAN:
                if q.step == "stats":
                    pool.wait_ge(var_ready, q.nth + 1)
                    nc.gpsimd.tensor_tensor(rstd[:, q.nth % 4, :], veps[:, q.nth % 4, :], mhalf[:, :],
                                            ALU.pow).then_inc(rstd_ready, 1)
                elif q.step == "project":
                    for t in range(2):
                        tile = q.proj // 2 + t
                        cols = slice(q.half * HT + t * BANK, q.half * HT + (t + 1) * BANK)
                        pool.wait_ge(rope_done, 2 * tile + 1)
                        if tile >= 2:
                            pool.wait_ge(key_ready, tile - 1)
                        nc.gpsimd.tensor_tensor(kR[:, tile % 2, :], rope1[:, (2 * tile) % 4, :],
                                                rope2[:, (2 * tile) % 4, :], ALU.add).then_inc(rope_sum, 1)
                        pool.wait_ge(rope_done, 2 * tile + 2)
                        nc.gpsimd.tensor_tensor(qT[:, cols], rope1[:, (2 * tile + 1) % 4, :], rope2[:, (2 * tile + 1) % 4, :],
                                                ALU.add).then_inc(rope_sum, 1)
                elif q.step == "bias":
                    n = q.layer
                    if q.kind == S:
                        pool.wait_ge(vec_loaded[n % 2], 16 * (n // 2 + 1))
                        if q.half == 0:
                            nc.gpsimd.tensor_tensor(b_both[:, :], vec[:, n % 2, 0, :], vec[:, n % 2, 1, :],
                                                    ALU.add).then_inc(both_ready, 1)
                        pool.wait_ge(res_ready, 2 * n + q.half + 1)
                    else:
                        pool.wait_ge(mid_ready, 2 * (2 * n + q.half + 1))
                    row = 0 if q.kind == S else 3
                    nc.gpsimd.tensor_tensor(half_of(x_bias, q.half), half_of(x_res, q.half),
                                            vec[:, n % 2, row:row + 1, :].broadcast_to([P, HC, P]),
                                            ALU.add).then_inc(bias_ready, 1)
            split_expert(pool, 0, w_even)

        @block.scalar
        def _(act):
            act.wait_ge(loaded, 16 * 7)
            for q in PLAN:
                if q.step == "turn":
                    if q.kind == T:
                        act.wait_ge(wt_loaded, 16 * (q.layer + 1))
                    elif q.kind == S and q.layer:
                        act.wait_ge(ws_loaded, 16 * q.layer)
                    for t in range(2):
                        u = q.turns + t
                        act.wait_ge(turn_full, u + 1)
                        src = turn[:, u % 2, :]
                        dst = xnT[:, q.half * HT + t * BANK:q.half * HT + (t + 1) * BANK]
                        if q.kind == E:
                            nc.scalar.activation(x_hi[:, q.half * HT + t * BANK:q.half * HT + (t + 1) * BANK], src, ACT.Copy)
                            nc.scalar.activation(dst, src, ACT.Copy).then_inc(turn_free[u % 2], 1)
                            continue
                        w = ws if q.kind == S else wt
                        if q.kind == T:
                            src = src.rearrange("d (t p) -> d p t", p=PATCH)
                            dst = xnT[:, q.half * HT:(q.half + 1) * HT].rearrange("d (p t) -> d p t", t=TIME)[
                                :, :, t * 8:(t + 1) * 8]
                        nc.scalar.activation(dst, src, ACT.Identity, bias=w[:, BETA:BETA + 1],
                                             scale=w[:, GAMMA:GAMMA + 1]).then_inc(turn_free[u % 2], 1)
                elif q.step == "values":
                    br = BRANCH[q.kind]
                    v = v_s if q.kind == S else v_t
                    if q.nth == 0:
                        act.wait_ge(ready, 9)
                    for t in range(2):
                        u = q.smalls + t
                        act.wait_ge(small_full, u + 1)
                        b0 = t * 8
                        for i in range(br.parts):
                            rows = slice(i * br.block, (i + 1) * br.block)
                            src = small[rows, u % 2, :].rearrange("p (u g d) -> p u g d", u=8, d=DH)
                            last = nc.scalar.activation(v[rows, b0:b0 + 8, :, i * VW:i * VW + DH], src, ACT.Copy)
                        last.then_inc(small_free[u % 2], 1)
                elif q.step == "part":
                    proj = STEPS["project", q.layer, q.kind, q.half, 0].proj
                    for t in range(2):
                        tile = proj // 2 + t
                        cols = slice(q.half * HT + t * BANK, q.half * HT + (t + 1) * BANK)
                        act.wait_ge(rope_sum, 2 * tile + 1)
                        for e in range(2):
                            last = nc.scalar.activation(kE[:, e, cols], kR[:, tile % 2, :], ACT.Copy, scale=hmask[:, e:e + 1])
                        last.then_inc(key_ready, 1)
                elif q.step in ("soft", "rest"):
                    i = STEPS["score", q.layer, q.kind, q.half, q.group].scores
                    h = int(q.step == "rest")
                    act.wait_ge(score_free, 2 * i + h + 1)
                    p = prob[:, i % 2, 2 * h:2 * h + 2, :, :].rearrange("p g k n -> p (g k n)")
                    nc.scalar.activation(p, p, ACT.Exp, scale=SCALE).then_inc(prob_ready, 1)
                elif q.step in ("head", "mix"):
                    h = int(q.step == "mix")
                    for k in range(2):
                        u = q.turns + k
                        act.wait_ge(turn_full, u + 1)
                        nc.scalar.activation(
                            probT[:, q.nth % 2, 2 * k:2 * k + 2, 2 * h:2 * h + 2, :].rearrange("p k g n -> p k (g n)"),
                            turn[:, u % 2, :].rearrange("p (k m) -> p k m", k=2), ACT.Copy).then_inc(turn_free[u % 2], 1)
                elif q.step == "out":
                    for t in range(2):
                        u = q.turns + t
                        act.wait_ge(turn_full, u + 1)
                        src = turn[:, u % 2, :]
                        dst = oT[:, q.half * HT + t * BANK:q.half * HT + (t + 1) * BANK]
                        if q.kind == T:
                            src = src.rearrange("d (p t) -> d t p", t=TIME)
                            dst = oT[:, q.half * HT:(q.half + 1) * HT].rearrange("d (t p) -> d t p", p=PATCH)[
                                :, :, t * 32:(t + 1) * 32]
                        nc.scalar.activation(dst, src, ACT.Copy).then_inc(turn_free[u % 2], 1)

        @block.tensor
        def _(pe):
            pe.wait_ge(loaded, 16 * 7)

            def turned(srcs, u):
                if u >= 2:
                    wait_read(pe, turn_free, u - 2)
                for j, src in enumerate(srcs):
                    last = nc.tensor.transpose(turn[:, u % 2, j * P:(j + 1) * P], src, ident[:, :])
                last.then_inc(turn_full, 1)

            def small_bank(u):
                if u >= 2:
                    wait_read(pe, small_free, u - 2)
                return small[:, u % 2, :]

            for q in PLAN:
                br = BRANCH.get(q.kind)
                w = ws if q.kind == S else wt
                n = br.block if br else 0
                if q.step == "turn":
                    normal = STEPS["normal", q.layer, q.kind, q.half, 0]
                    for t in range(2):
                        pe.wait_ge(nrm_ready, 2 * normal.nth + t + 1)
                        c0 = q.half * HC + 4 * t
                        turned([x_nrm[:, c, :] for c in range(c0, c0 + 4)], q.turns + t)
                elif q.step == "values":
                    for t in range(2):
                        bank = small_bank(q.smalls + t)
                        for v in range(8):
                            b = q.half * 16 + t * 8 + v
                            for i in range(br.parts):
                                if q.kind == S:
                                    tok = b * n
                                else:
                                    tok = (2 * (b // 4) + i // 2) * P + (b % 4) * n
                                h = i % 2
                                last = nc.tensor.matmul(bank[i * n:(i + 1) * n, v * 64:(v + 1) * 64], xnT[:, tok:tok + n],
                                                        w[:, WV + 64 * h:WV + 64 * h + 64], start=True, stop=True)
                        last.then_inc(small_full, 1)
                elif q.step == "project":
                    if q.scores:
                        pe.wait_ge(score_free, 2 * q.scores)
                    turn_step = STEPS["turn", q.layer, q.kind, q.half, 0]
                    for t in range(2):
                        wait_read(pe, turn_free, turn_step.turns + t)
                    for t in range(2):
                        cols = xnT[:, q.half * HT + t * BANK:q.half * HT + (t + 1) * BANK]
                        for j, off in enumerate((WK, WQ)):
                            i = q.proj + 2 * t + j
                            if i >= 4:
                                pe.wait_ge(proj_free, i - 3)
                            nc.tensor.matmul(score[:, i % 4, :], w[:, off:off + P], cols, start=True,
                                             stop=True).then_inc(proj_full, 1)
                elif q.step == "score":
                    proj = STEPS["project", q.layer, q.kind, q.half, 0]
                    tiles = 1 if q.kind == S and q.group == 0 else 2
                    pe.wait_ge(rope_sum, proj.proj + 2 * tiles)
                    pe.wait_ge(key_ready, proj.proj // 2 + tiles)
                    pe.wait_ge(proj_free, q.proj)
                    if q.scores:
                        pe.wait_ge(score_free, 2 * q.scores)
                    for h in range(2):
                        pairs = range(2 * h, 2 * h + 2)
                        if q.kind == T:
                            for g in pairs:
                                nc.tensor.matmul(score[:, g, :], pmask[:, 0:P], pmask[:, P:P + BANK], start=True, stop=False,
                                                 skip_group_check=True)
                        for c in range(br.group_chunks):
                            chunk = q.half * HC + q.group * br.group_chunks + c
                            for b in range(br.blocks):
                                tok = chunk * P + b * n
                                for g in pairs:
                                    rows = slice(32 * g, 32 * g + 32)
                                    last = nc.tensor.matmul(
                                        score[b * n:(b + 1) * n, g, c * 2 * n:(c + 1) * 2 * n], qT[rows, tok:tok + n],
                                        kE[rows, :, tok:tok + n], start=q.kind == S, stop=True,
                                        skip_group_check=q.kind == T, tile_position=(32 * g, b * n))
                        last.then_inc(score_full, 1)
                elif q.step == "head":
                    i = STEPS["score", q.layer, q.kind, q.half, q.group].scores
                    pe.wait_ge(prob_ready, 2 * i + 1)
                    for z in range(2):
                        turned([prob[:, i % 2, g, k, :] for k in (2 * z, 2 * z + 1) for g in (0, 1)], q.turns + z)
                elif q.step == "mix":
                    i = STEPS["score", q.layer, q.kind, q.half, q.group].scores
                    head = STEPS["head", q.layer, q.kind, q.half, q.group]
                    values = STEPS["values", q.layer, q.kind, q.half, 0]
                    v = v_s if q.kind == S else v_t
                    per_unit = 2 if q.kind == S else 1

                    def weighted(k, h):
                        wait_read(pe, turn_free, (head if h == 0 else q).turns + k // 2)
                        unit = q.smalls + k // per_unit
                        bank = small_bank(unit) if h == 0 and k % per_unit == 0 else small[:, unit % 2, :]
                        blk0 = (q.group * 4 + k) * 2 if q.kind == S else k * 4
                        cols = bank[:, 0:16 * VW].rearrange("p (c g w) -> p c g w", c=2, g=PAIRS)
                        if q.kind == S:
                            cols = cols[:, k % 2:k % 2 + 1, :, :]
                        for b in range(br.blocks):
                            for g in (2 * h, 2 * h + 1):
                                last = nc.tensor.matmul(
                                    cols[b * n:(b + 1) * n, :, g, :],
                                    probT[:, q.nth % 2, k, g, b * n:(b + 1) * n], v[:, blk0 + b, g, :], start=True, stop=True)
                        if h == 1 and k % per_unit == per_unit - 1:
                            last.then_inc(small_full, 1)

                    wait_read(pe, small_free, values.smalls)
                    wait_read(pe, small_free, values.smalls + 1)
                    ahead = range(2 * per_unit)
                    for k in ahead:
                        weighted(k, 0)
                    pe.wait_ge(prob_ready, 2 * i + 2)
                    for z in range(2):
                        turned([prob[:, i % 2, g, k, :] for k in (2 * z, 2 * z + 1) for g in (2, 3)], q.turns + z)
                    for k in ahead:
                        weighted(k, 1)
                    for k in range(len(ahead), 4):
                        weighted(k, 0)
                        weighted(k, 1)
                elif q.step == "out":
                    mix = STEPS["mix", q.layer, q.kind, q.half, br.groups - 1]
                    units = 2 if q.kind == S else 4
                    for z in range(units - 2, units):
                        wait_read(pe, small_free, mix.smalls + z)
                    for t in range(2):
                        turned([o_nrm[:, c // 2, (c % 2) * P:(c % 2 + 1) * P] for c in range(4 * t, 4 * t + 4)],
                               q.turns + t)
                    for t in range(2):
                        if q.kind == T:
                            wait_read(pe, turn_free, q.turns + 1)
                        wait_read(pe, turn_free, q.turns + t)
                        bank = small_bank(q.smalls + t)
                        for j in range(4):
                            c = q.half * HC + 4 * t + j
                            last = nc.tensor.matmul(bank[:, j * P:(j + 1) * P], oT[:, c * P:(c + 1) * P], w[:, WO:WO + P],
                                                    start=True, stop=True)
                        last.then_inc(small_full, 1)
                elif q.step == "logits":
                    turn_step = STEPS["turn", q.layer, E, q.half, 0]
                    for t in range(2):
                        wait_read(pe, turn_free, turn_step.turns + t)
                    bank = small_bank(q.smalls)
                    for c in range(HC):
                        last = nc.tensor.matmul(bank[:, c * EXPERTS:(c + 1) * EXPERTS],
                                                xnT[:, (q.half * HC + c) * P:(q.half * HC + c + 1) * P], rt[:, :],
                                                start=True, stop=True)
                    last.then_inc(small_full, 1)

        @block.vector
        def _(dve):
            moments = 0
            finals = 0

            def moments_of(src, half, t, done):
                for c in range(4 * t, 4 * t + 4):
                    nc.vector.bn_stats(stats[:, c, :], src[:, half * HC + c, :]).then_inc(stat_done, 1)
                return done + 4

            for q in PLAN:
                if q.step == "stats":
                    if q.kind == C:
                        dve.wait_ge(x_loaded[q.half], 16)
                    if q.kind == E:
                        nc.vector.tensor_tensor(half_of(x_in, q.half), half_of(x_in, q.half), half_of(x_res, q.half),
                                                ALU.add).then_inc(add_ready, 1)
                        dve.wait_ge(add_ready, q.half + 1)
                    src = {C: x_in, S: x_res, T: x_mid, F: x_sum, E: x_in}[q.kind]
                    slot = q.nth % 4
                    if q.kind not in (T, F):
                        moments = moments_of(src, q.half, 0, moments)
                        moments = moments_of(src, q.half, 1, moments)
                    dve.wait_ge(stat_done, moments)
                    for c in range(HC):
                        nc.vector.bn_aggr(mv[:, slot, c, :], stats[:, c, :]).then_inc(stat_done, 1)
                    moments += HC
                    dve.wait_ge(stat_done, moments)
                    eps = CONV_EPS if q.kind == C else NORM_EPS
                    nc.vector.tensor_scalar(veps[:, slot, :], mv[:, slot, :, 1], eps, None, ALU.add).then_inc(var_ready, 1)
                    if q.kind == T:
                        out_step = STEPS["out", q.layer, S, q.half, 0]
                        for t in range(2):
                            u = out_step.smalls + t
                            c0 = q.half * HC + 4 * t
                            nc.vector.tensor_tensor(x_sum[:, c0:c0 + 4, :], small[:, u % 2, :].rearrange("p (c n) -> p c n", n=P),
                                                    b_both[:, None, :].broadcast_to([P, 4, P]),
                                                    ALU.add).then_inc(small_free[u % 2], 1)
                    if q.kind == F:
                        for c in range(HC):
                            k = q.half * HC + c
                            last = nc.vector.scalar_tensor_tensor(
                                out=x_nrm[:, k, :], in0=x_sum[:, k, :], scalar=mv[:, slot, c, 0:1],
                                in1=vec[:, q.layer % 2, 2, :], op0=ALU.subtract, op1=ALU.mult)
                        last.then_inc(fin_step, 1)
                elif q.step == "normal":
                    stat = STEPS["stats", q.layer, q.kind, q.half, 0]
                    slot = stat.nth % 4
                    src = {C: x_in, S: x_res, T: x_mid, E: x_in}[q.kind]
                    dst = x_res if q.kind == C else x_nrm
                    dve.wait_ge(rstd_ready, stat.nth + 1)
                    for c in range(HC):
                        k = q.half * HC + c
                        last = nc.vector.tensor_scalar(dst[:, k, :], src[:, k, :], mv[:, slot, c, 0:1],
                                                       rstd[:, slot, c:c + 1], ALU.subtract, ALU.mult)
                        if c % 4 == 3:
                            last.then_inc(nrm_ready, 1)
                    if q.kind == C:
                        dve.wait_ge(nrm_ready, 2 * q.nth + 2)
                        dve.sem_inc(res_ready, 1)
                elif q.step == "final":
                    stat = STEPS["stats", q.layer, F, q.half, 0]
                    slot = stat.nth % 4
                    finals += 1
                    dve.wait_ge(fin_step, finals)
                    dve.wait_ge(rstd_ready, stat.nth + 1)
                    dve.wait_ge(bias_ready, STEPS["bias", q.layer, F, q.half, 0].nth + 1)
                    for c in range(HC):
                        k = q.half * HC + c
                        last = nc.vector.scalar_tensor_tensor(
                            out=x_res[:, k, :], in0=x_nrm[:, k, :], scalar=rstd[:, slot, c:c + 1],
                            in1=x_bias[:, k, :], op0=ALU.mult, op1=ALU.add)
                    last.then_inc(res_ready, 1)
                    dve.wait_ge(res_ready, 2 + 2 * q.layer + q.half + 1)
                elif q.step == "turn" and q.nth == 0:
                    dve.wait_ge(ready, 3)
                    for br, v in ((SPATIAL, v_s), (TEMPORAL, v_t)):
                        for i in range(br.parts):
                            nc.vector.memset(v[i * br.block:(i + 1) * br.block, :, :, i * VW + DH:(i + 1) * VW],
                                             1.0).then_inc(ready, 1)
                    dve.wait_ge(loaded, 16 * 7)
                elif q.step == "project":
                    table, length = (cs_s, PATCH) if q.kind == S else (cs_t, TIME)
                    def by_sine(i):
                        dve.wait_ge(swapped, i + 1)
                        z = rope2[:, i % 4, :].rearrange("p (s n) -> p s n", n=length)
                        nc.vector.tensor_tensor(z, z, table[:, 1, None, :].broadcast_to([P, BANK // length, length]),
                                                ALU.mult).then_inc(rope_done, 1)

                    for j in range(4):
                        i = q.proj + j
                        if i >= 4:
                            dve.wait_ge(rope_sum, i - 3)
                        dve.wait_ge(proj_full, i + 1)
                        nc.vector.stream_shuffle(rope2[:, i % 4, :], score[:, i % 4, :], SWAP).then_inc(swapped, 1)
                        nc.vector.tensor_tensor(
                            rope1[:, i % 4, :].rearrange("p (s n) -> p s n", n=length),
                            score[:, i % 4, :].rearrange("p (s n) -> p s n", n=length),
                            table[:, 0, None, :].broadcast_to([P, BANK // length, length]), ALU.mult).then_inc(proj_free, 1)
                        if q.kind == T or j < 2:
                            by_sine(i)
                    if q.kind == S:
                        by_sine(q.proj + 2)
                        by_sine(q.proj + 3)
                elif q.step in ("soft", "rest"):
                    i = STEPS["score", q.layer, q.kind, q.half, q.group].scores
                    h = int(q.step == "rest")
                    block_len = BRANCH[q.kind].block
                    per = BANK // block_len
                    dve.wait_ge(score_full, 2 * i + h + 1)
                    mine = score[:, 2 * h:2 * h + 2, :].rearrange("p g (r n) -> p (g r) n", n=block_len)
                    tops = top[:, i % 2, h, 0:2 * per]
                    nc.vector.tensor_reduce(tops, mine, AX_X, ALU.max).then_inc(top_ready, 1)
                    dve.wait_ge(top_ready, 2 * i + h + 1)
                    nc.vector.tensor_tensor(
                        prob[:, i % 2, 2 * h:2 * h + 2, :, :].rearrange("p g k (r n) -> p (g k r) n", n=block_len),
                        mine, tops[:, :, None].broadcast_to([P, 2 * per, block_len]),
                        ALU.subtract).then_inc(score_free, 1)
                elif q.step == "divide":
                    mix = STEPS["mix", q.layer, q.kind, q.half, q.group if q.kind == S else 0]
                    first = mix.smalls + (0 if q.kind == S else 2 * q.group)
                    for z in range(2):
                        u = first + z
                        dve.wait_ge(small_full, u + 1)
                        src = small[:, u % 2, 0:16 * VW].rearrange("p (h d) -> p h d", d=VW)
                        nc.vector.reciprocal(den[:, u % 2, :], src[:, :, DH]).then_inc(den_ready, 1)
                        dve.wait_ge(den_ready, 2 * q.nth + z + 1)
                        nc.vector.tensor_tensor(o_nrm[:, q.group * 2 + z, :].rearrange("p (h d) -> p h d", d=DH),
                                                src[:, :, 0:DH], den[:, u % 2, :, None].broadcast_to([P, 16, DH]),
                                                ALU.mult).then_inc(small_free[u % 2], 1)
                elif q.step == "out" and q.kind == S:
                    dve.wait_ge(bias_ready, STEPS["bias", q.layer, S, q.half, 0].nth + 1)
                    dve.wait_ge(both_ready, q.layer + 1)
                    for t in range(2):
                        u = q.smalls + t
                        c0 = q.half * HC + 4 * t
                        dve.wait_ge(small_full, u + 1)
                        src = small[:, u % 2, :].rearrange("p (c n) -> p c n", n=P)
                        nc.vector.tensor_tensor(x_mid[:, c0:c0 + 4, :], src, x_bias[:, c0:c0 + 4, :], ALU.add).then_inc(mid_ready, 1)
                        dve.wait_ge(mid_ready, 2 * (2 * q.layer + q.half) + t + 1)
                        moments = moments_of(x_mid, q.half, t, moments)
                elif q.step == "out":
                    for t in range(2):
                        u = q.smalls + t
                        c0 = q.half * HC + 4 * t
                        dve.wait_ge(small_full, u + 1)
                        z = flat(x_sum[:, c0:c0 + 4, :])
                        nc.vector.tensor_tensor(z, small[:, u % 2, :], z, ALU.add).then_inc(small_free[u % 2], 1)
                        wait_read(dve, small_free, u)
                        moments = moments_of(x_sum, q.half, t, moments)
                elif q.step == "split":
                    turn_step = STEPS["turn", q.layer, E, q.half, 0]
                    for t in range(2):
                        wait_read(dve, turn_free, turn_step.turns + t)
                        cols = slice(q.half * HT + t * BANK, q.half * HT + (t + 1) * BANK)
                        nc.vector.tensor_tensor(x_lo[:, cols], xnT[:, cols], x_hi[:, cols].bitcast(F32),
                                                ALU.subtract).then_inc(split_done, 1)
                elif q.step == "logits":
                    dve.wait_ge(small_full, q.smalls + 1)
                    nc.vector.tensor_copy(logit[:, q.half * HC:(q.half + 1) * HC, :],
                                          small[:, q.smalls % 2, 0:HC * EXPERTS].rearrange("p (c e) -> p c e", e=EXPERTS)
                                          ).then_inc(small_free[q.smalls % 2], 1)
                    wait_read(dve, small_free, q.smalls)

        layers.close()

        w_odd = sb("w_odd", [P, 2, 2, FF], F32R)
        hid = sb("hid", [P, FC, BANK])
        h_hi = sb("h_hi", [P, 2, FC, BANK], F32R)
        h_lo = sb("h_lo", [P, 2, FC, BANK], F32R)
        gate = sb("gate", [P, EXPERTS, CHUNKS])
        lg = sb("lg", [P, CHUNKS, EXPERTS])
        lmax = sb("lmax", [P, CHUNKS])
        lsum = sb("lsum", [P, CHUNKS])
        prb = sb("prb", [P, CHUNKS, EXPERTS])
        above = sb("above", [P, HC, EXPERTS, EXPERTS])
        before = sb("before", [P, EXPERTS, EXPERTS])
        rank = sb("rank", [P, CHUNKS, EXPERTS])
        ties = sb("ties", [P, CHUNKS, EXPERTS])
        gateT = sb("gateT", [P, P])
        gates = sb("gates", [P, EXPERTS, TOKENS])
        gated = sb("gated", [P, 4, BANK])
        y_sum = sb("y_sum", [P, TOKENS])
        kept = nc.dram_tensor("gates_kept", (EXPERTS * CHUNKS, P), F32).ap()
        TILES = TOKENS // BANK
        STEPS_E = EXPERTS * TILES
        w_slot = (w_even, w_odd)
        ybank = (small[:, 0, :], small[:, 1, :], turn[:, 0, :], turn[:, 1, :])

        block = ctx.enter_context(nc.Block())

        @block.sync
        def _(sp):
            load_expert(sp, 1)
            sp.wait_ge(gates_out, 1)
            sp.dma_start(kept, gateT[:, :]).then_inc(gates_kept, 16)
            sp.wait_ge(gates_kept, 16)
            rows = kept.rearrange("(e c) t -> e (c t)", e=EXPERTS)
            for t in range(TILES):
                cols = slice(t * BANK, (t + 1) * BANK)
                sp.dma_start(gates[:, 0, cols], rows[0:1, cols].broadcast_to([P, BANK])).then_inc(first_gates[t], 16)
            for e in range(1, EXPERTS):
                row = rows[e:e + 1]
                sp.dma_start(gates[:, e, :], row.broadcast_to([P, TOKENS])).then_inc(gate_loaded[e], 16)
                if e >= 2:
                    load_expert(sp, e)
            for t in range(TILES):
                sp.wait_ge(out_ready, t + 1)
                sp.dma_start(out[:, 4 * t:4 * t + 4, :], x_in[:, 4 * t:4 * t + 4, :]).then_inc(stored, 16)
            sp.wait_ge(stored, 16 * TILES)

        @block.gpsimd
        def _(pool):
            split_expert(pool, 1, w_odd)
            for n in range(STEPS_E):
                e, t = n // TILES, n % TILES
                done = (n + 2) // TILES
                if t == TILES - 2 and done + 1 < EXPERTS:
                    pool.wait_ge(y_full, TILES * done)
                    split_expert(pool, done + 1, w_slot[(done + 1) % 2])
                if e:
                    cols = slice(t * BANK, (t + 1) * BANK)
                    pool.wait_ge(y_gated, n + 1)
                    nc.gpsimd.tensor_tensor(y_sum[:, cols], y_sum[:, cols], gated[:, n % 4, :], ALU.add).then_inc(y_added, 1)

        @block.scalar
        def _(act):
            act.wait_ge(lg_sub, 1)
            nc.scalar.activation(prb[:, :, :], lg[:, :, :], ACT.Exp).then_inc(lg_exp, 1)
            for n in range(STEPS_E):
                if n == 3:
                    act.wait_ge(gates_turned, 1)
                    nc.scalar.activation(gateT[:, :], ybank[3][:, 0:P], ACT.Copy).then_inc(gates_out, 1)
                if n >= 2:
                    act.wait_ge(y_full, n - 1)
                for c in range(FC):
                    b = n * FC + c
                    if n:
                        act.wait_ge(lo_ready, b - FC + 1)
                    act.wait_ge(h_full, b + 1)
                    nc.scalar.activation(hid[:, c, :], score[:, c, :], ACT.Gelu)
                    nc.scalar.activation(h_hi[:, n % 2, c, :], score[:, c, :], ACT.Gelu).then_inc(h_ready, 1)

        @block.tensor
        def _(pe):
            def first(n):
                e, t = n // TILES, n % TILES
                w = w_slot[e % 2]
                cols = slice(t * BANK, (t + 1) * BANK)
                if t == 0:
                    pe.wait_ge(w_split, e + 1)
                if n < TILES:
                    pe.wait_ge(split_done, t + 1)
                for c in range(FC):
                    if n >= 1:
                        pe.wait_ge(h_ready, (n - 1) * FC + c + 1)
                    m = slice(c * P, (c + 1) * P)
                    nc.tensor.matmul(score[:, c, :], w[:, 0, 0, m], x_hi[:, cols], start=True, stop=False)
                    nc.tensor.matmul(score[:, c, :], w[:, 0, 0, m], x_lo[:, cols], start=False, stop=False)
                    nc.tensor.matmul(score[:, c, :], w[:, 1, 0, m], x_hi[:, cols], start=False, stop=True).then_inc(h_full, 1)

            def second(n):
                w = w_slot[n // TILES % 2]
                if n >= 4:
                    pe.wait_ge(y_gated, n - 3)
                if n == 3:
                    pe.wait_ge(gates_out, 1)
                for c in range(FC):
                    m = slice(c * P, (c + 1) * P)
                    pe.wait_ge(h_ready, n * FC + c + 1)
                    nc.tensor.matmul(ybank[n % 4], w[:, 0, 1, m], h_hi[:, n % 2, c, :], start=c == 0, stop=False)
                    nc.tensor.matmul(ybank[n % 4], w[:, 1, 1, m], h_hi[:, n % 2, c, :], start=False, stop=False)
                    pe.wait_ge(lo_ready, n * FC + c + 1)
                    last = nc.tensor.matmul(ybank[n % 4], w[:, 0, 1, m], h_lo[:, n % 2, c, :], start=False, stop=c == FC - 1)
                last.then_inc(y_full, 1)

            def turn_sum(t):
                pe.wait_ge(y_added, STEPS_E - TILES - TILES + t + 1)
                pe.wait_ge(h_ready, STEPS_E * FC - FC + t + 1)
                for j in range(4):
                    c = 4 * t + j
                    last = nc.tensor.transpose(score[:, t, j * P:(j + 1) * P], y_sum[:, c * P:(c + 1) * P], ident[:, :])
                last.then_inc(sum_turned, 1)

            first(0)
            for n in range(1, STEPS_E):
                first(n)
                if n == 2:
                    pe.wait_ge(route, ROUTE_LINKS)
                    nc.tensor.transpose(ybank[3][:, 0:P], gate[:, :, :].rearrange("p e c -> p (e c)"),
                                        ident[:, :]).then_inc(gates_turned, 1)
                second(n - 1)
            turn_sum(0)
            turn_sum(1)
            second(STEPS_E - 1)
            turn_sum(2)
            turn_sum(3)

        @block.vector
        def _(dve):
            links = [0]

            def link(ins):
                links[0] += 1
                ins.then_inc(route, 1)
                dve.wait_ge(route, links[0])

            def rank_half(half):
                c = slice(half * HC, (half + 1) * HC)
                square = [P, HC, EXPERTS, EXPERTS]
                mine = lg[:, c, :, None].broadcast_to(square)
                others = lg[:, c, None, :].broadcast_to(square)
                link(nc.vector.tensor_tensor(above[:, :, :, :], others, mine, ALU.is_gt))
                link(nc.vector.tensor_reduce(rank[:, c, :], above[:, :, :, :], AX_X, ALU.add))
                link(nc.vector.tensor_tensor(above[:, :, :, :], others, mine, ALU.is_equal))
                link(nc.vector.tensor_tensor(above[:, :, :, :], above[:, :, :, :],
                                             before[:, None, :, :].broadcast_to(square), ALU.mult))
                link(nc.vector.tensor_reduce(ties[:, c, :], above[:, :, :, :], AX_X, ALU.add))
                link(nc.vector.tensor_tensor(rank[:, c, :], rank[:, c, :], ties[:, c, :], ALU.add))
                link(nc.vector.tensor_scalar(rank[:, c, :], rank[:, c, :], 1.5, None, ALU.is_lt))
                link(nc.vector.tensor_tensor(gate[:, :, c].rearrange("p e c -> p c e"), lg[:, c, :], rank[:, c, :], ALU.mult))

            every = [P, CHUNKS, EXPERTS]
            link(nc.vector.tensor_reduce(lmax[:, :], logit[:, :, :], AX_X, ALU.max))
            nc.vector.tensor_tensor(lg[:, :, :], logit[:, :, :], lmax[:, :, None].broadcast_to(every),
                                    ALU.subtract).then_inc(lg_sub, 1)
            for e in range(EXPERTS):
                if e:
                    nc.vector.memset(before[:, e, 0:e], 1.0)
                nc.vector.memset(before[:, e, e:EXPERTS], 0.0)
            dve.wait_ge(lg_exp, 1)
            link(nc.vector.tensor_reduce(lsum[:, :], prb[:, :, :], AX_X, ALU.add))
            link(nc.vector.reciprocal(lmax[:, :], lsum[:, :]))
            link(nc.vector.tensor_tensor(lg[:, :, :], prb[:, :, :], lmax[:, :, None].broadcast_to(every), ALU.mult))

            def gated_outputs(n):
                e, t = n // TILES, n % TILES
                cols = slice(t * BANK, (t + 1) * BANK)
                if e == 0:
                    dve.wait_ge(first_gates[t], 16)
                elif t == 0:
                    dve.wait_ge(gate_loaded[e], 16)
                if n >= TILES + 4:
                    dve.wait_ge(y_added, n - TILES - 3)
                dve.wait_ge(y_full, n + 1)
                dst = y_sum[:, cols] if e == 0 else gated[:, n % 4, :]
                nc.vector.tensor_tensor(dst, ybank[n % 4], gates[:, e, cols], ALU.mult).then_inc(y_gated, 1)

            gated_tiles = 0
            for n in range(STEPS_E):
                for c in range(FC):
                    b = n * FC + c
                    dve.wait_ge(h_ready, b + 1)
                    nc.vector.tensor_tensor(h_lo[:, n % 2, c, :], hid[:, c, :], h_hi[:, n % 2, c, :].bitcast(F32),
                                            ALU.subtract).then_inc(lo_ready, 1)
                if n == 0:
                    rank_half(0)
                    rank_half(1)
                while gated_tiles < (n - 2 if n < STEPS_E - 4 else n):
                    gated_outputs(gated_tiles)
                    gated_tiles += 1
            gated_outputs(STEPS_E - 1)
            for t in range(TILES):
                dve.wait_ge(sum_turned, t + 1)
                dst = flat(x_in[:, 4 * t:4 * t + 4, :])
                nc.vector.tensor_tensor(dst, score[:, t, :], dst, ALU.add).then_inc(out_ready, 1)

def rope_table(length):
    import numpy as np
    freq = (1.0 / np.float32(10000.0) ** (np.arange(0, DH, 2, dtype=np.float32) / np.float32(DH))).astype(np.float32)
    angle = (np.arange(length, dtype=np.float32)[:, None] * freq[None, :]).astype(np.float32)
    angle = np.repeat(angle, 2, axis=-1).T
    sign = np.where(np.arange(DH) % 2 == 0, -1.0, 1.0)[:, None]
    cos = np.tile(np.cos(angle.astype(np.float64)), (HEADS, 1))
    sin = np.tile(np.sin(angle.astype(np.float64)) * sign, (HEADS, 1))
    return np.ascontiguousarray(np.stack([cos, sin], axis=1).astype(np.float32))


def kernel(**inputs):
    import numpy as np
    import concourse.bacc as bacc
    from concourse.bass_utils import run_bass_kernel_spmd

    a = {k: np.asarray(v) for k, v in inputs.items()}

    def packed(tag):
        qkv = a[f"L0_conv_w_qkv_{tag}"]
        q, k, v = qkv[:, :, 0:P], qkv[:, :, P:2 * P], qkv[:, :, 2 * P:3 * P]
        v = v.reshape(DEPTH, P, PAIRS, 2, DH).transpose(0, 1, 3, 2, 4).reshape(DEPTH, P, P)
        w = np.concatenate([q, k, v, a[f"L0_conv_w_out_{tag}"],
                            a[f"L0_conv_ln_{tag}_g"][:, :, None], a[f"L0_conv_ln_{tag}_b"][:, :, None]], axis=2)
        return np.ascontiguousarray(w)

    parity = np.zeros((2, P + BANK), np.float32)
    for r in range(2):
        parity[r, 0:P] = (np.arange(P) // TIME) % 2 == r
        parity[r, P:] = np.where((np.arange(BANK) // TIME) % 2 == r, 0.0, -1e30)
    import ml_dtypes
    arrays = {
        "x": np.ascontiguousarray(a["x"].reshape(CHUNKS, P, P).transpose(1, 0, 2)),
        "w_s": packed("s"),
        "w_t": packed("t"),
        "vec_in": np.ascontiguousarray(np.stack([a["L0_conv_b_out_s"], a["L0_conv_b_out_t"], a["L0_conv_ln_f_g"],
                                                 a["L0_conv_ln_f_b"]], axis=1)),
        "rope_s": rope_table(PATCH),
        "rope_t": rope_table(TIME),
        "headmask": np.ascontiguousarray(np.stack([(np.arange(P) // DH) % 2 == e for e in range(2)], axis=1).astype(np.float32)),
        "ident": np.eye(P, dtype=np.float32),
        "pairmask": parity.astype(ml_dtypes.bfloat16),
        "router": np.ascontiguousarray(a["L0_ffn_Wr"]),
        "w1": np.ascontiguousarray(a["L0_ffn_W1"]),
        "w2": np.ascontiguousarray(a["L0_ffn_W2"].reshape(EXPERTS, FC, P, P).transpose(0, 2, 1, 3)),
    }
    nc = bacc.Bacc("TRN2", target_bir_lowering=False, num_devices=1)
    args = [nc.dram_tensor(f"in_{k}", v.shape, mybir.dt.from_np(v.dtype), kind="ExternalInput").ap()
            for k, v in arrays.items()]
    out = nc.dram_tensor("out_x", (P, CHUNKS, P), F32, kind="ExternalOutput").ap()
    metaformer(nc, *args, out)
    r = run_bass_kernel_spmd(nc, [{f"in_{k}": v for k, v in arrays.items()}], core_ids=[0])
    got = r.results[0]["out_x"]
    return np.ascontiguousarray(got.transpose(1, 0, 2)).reshape(BATCH, TIME, PATCH, P)
```
